# Optimizing a Trainium2 kernel written in Bass

```python
import numpy as np
import jax
import jax.numpy as jnp

def _softmax(x, axis=-1):
    return jax.nn.softmax(x, axis=axis)

def _gelu(x):
    return jax.nn.gelu(x, approximate=True)

def _silu(x):
    return jax.nn.silu(x)

def _sigmoid(x):
    return jax.nn.sigmoid(x)

def _layernorm(x, axis=-1, eps=1e-05):
    m = jnp.mean(x, axis=axis, keepdims=True)
    v = jnp.var(x, axis=axis, keepdims=True)
    return (x - m) / jnp.sqrt(v + eps)

def _scatter_add(tgt, idx, src, axis=0):
    return tgt.at[idx].add(src)

def _segment_sum(src, seg, n):
    return jax.ops.segment_sum(src, seg, n)
kernel_name = 'mk_adj_resnorm_d2_adj_r2_c1e9f7'

def setup_inputs(seed: int=0):
    np.random.seed(seed)
    _w = jnp.asarray

    def _rec_inputs():
        import jax
        import jax.numpy as jnp
        _gk = jax.random.key(seed)
        x = 7.22e-05 + 1 * jax.random.normal(jax.random.fold_in(_gk, 1), (16, 512, 256), jnp.float32)
        _a = jax.random.bernoulli(jax.random.fold_in(_gk, 2), 0.015625, (16, 512, 512))
        adj = _a.astype(jnp.int32)
        return (x, adj)
    x, adj = _rec_inputs()

    def _L0_gnn_setup():
        import jax, jax.numpy as jnp
        import numpy as np
        EMBED_DIM = 256
        N_HEADS = 8
        HEAD_DIM = EMBED_DIM // N_HEADS
        NEG_INF = -1000000000.0
        key = jax.random.key(seed)
        ks = jax.random.split(key, 10)
        bs, n_agents = (64, 128)
        inputs = jax.random.normal(ks[0], (bs, n_agents, EMBED_DIM), dtype=jnp.float32)
        adj = jax.random.randint(ks[1], (bs, n_agents, n_agents), 0, 2, dtype=jnp.int32)
        s = 1.0 / np.sqrt(EMBED_DIM)
        Wq = jax.random.normal(ks[2], (EMBED_DIM, EMBED_DIM), dtype=jnp.float32) * s
        Wk = jax.random.normal(ks[3], (EMBED_DIM, EMBED_DIM), dtype=jnp.float32) * s
        Wv = jax.random.normal(ks[4], (EMBED_DIM, EMBED_DIM), dtype=jnp.float32) * s
        Wo = jax.random.normal(ks[5], (EMBED_DIM, EMBED_DIM), dtype=jnp.float32) * s
        bq = jnp.zeros((EMBED_DIM,), jnp.float32)
        bk = jnp.zeros((EMBED_DIM,), jnp.float32)
        bv = jnp.zeros((EMBED_DIM,), jnp.float32)
        bo = jnp.zeros((EMBED_DIM,), jnp.float32)
        return {'inputs': inputs, 'adj': adj, 'Wq': Wq, 'bq': bq, 'Wk': Wk, 'bk': bk, 'Wv': Wv, 'bv': bv, 'Wo': Wo, 'bo': bo}
    _L0_gnn_all = _L0_gnn_setup()
    _L0_gnn_in = {k: v for k, v in _L0_gnn_all.items() if k in ('Wq', 'bq', 'Wk', 'bk', 'Wv', 'bv', 'Wo', 'bo')}
    del _L0_gnn_all

    def _L1_gnn_setup():
        import jax, jax.numpy as jnp
        import numpy as np
        ALPHA = 0.2
        NEG_INF = -1000000000.0
        key = jax.random.key(seed)
        k1, k2, k3, k4, k5 = jax.random.split(key, 5)
        B, N, F_IN, F_OUT = (16, 512, 256, 256)
        graph_input = jax.random.normal(k1, (B, N, F_IN), dtype=jnp.float32)
        adj = jax.random.randint(k2, (B, N, N), 0, 2, dtype=jnp.int32)
        W = jax.random.normal(k3, (F_OUT, F_IN), dtype=jnp.float32) * (1.414 / np.sqrt(F_IN))
        a1 = jax.random.normal(k4, (F_OUT, 1), dtype=jnp.float32) * 0.1
        a2 = jax.random.normal(k5, (F_OUT, 1), dtype=jnp.float32) * 0.1
        return {'graph_input': graph_input, 'adj': adj, 'W': W, 'a1': a1, 'a2': a2}
    _L1_gnn_all = _L1_gnn_setup()
    _L1_gnn_in = {k: v for k, v in _L1_gnn_all.items() if k in ('W', 'a1', 'a2')}
    del _L1_gnn_all
    return {'x': x, 'adj': adj, 'L0_gnn_Wq': _L0_gnn_in['Wq'], 'L0_gnn_bq': _L0_gnn_in['bq'], 'L0_gnn_Wk': _L0_gnn_in['Wk'], 'L0_gnn_bk': _L0_gnn_in['bk'], 'L0_gnn_Wv': _L0_gnn_in['Wv'], 'L0_gnn_bv': _L0_gnn_in['bv'], 'L0_gnn_Wo': _L0_gnn_in['Wo'], 'L0_gnn_bo': _L0_gnn_in['bo'], 'L1_gnn_W': _L1_gnn_in['W'], 'L1_gnn_a1': _L1_gnn_in['a1'], 'L1_gnn_a2': _L1_gnn_in['a2']}

def reference(x, adj, L0_gnn_Wq, L0_gnn_bq, L0_gnn_Wk, L0_gnn_bk, L0_gnn_Wv, L0_gnn_bv, L0_gnn_Wo, L0_gnn_bo, L1_gnn_W, L1_gnn_a1, L1_gnn_a2):
    import jax
    import jax.numpy as jnp

    def _L0_gnn_ref(inputs, adj, Wq, bq, Wk, bk, Wv, bv, Wo, bo):
        import jax, jax.numpy as jnp
        import numpy as np
        EMBED_DIM = 256
        N_HEADS = 8
        HEAD_DIM = EMBED_DIM // N_HEADS
        NEG_INF = -1000000000.0
        bs, n, _ = inputs.shape
        q = (inputs @ Wq + bq).reshape(bs, n, N_HEADS, HEAD_DIM)
        k = (inputs @ Wk + bk).reshape(bs, n, N_HEADS, HEAD_DIM)
        v = (inputs @ Wv + bv).reshape(bs, n, N_HEADS, HEAD_DIM)
        logits = jnp.einsum('bqhd,bkhd->bhqk', q, k) / np.sqrt(HEAD_DIM)
        mask = (adj > 0)[:, None, :, :]
        logits = jnp.where(mask, logits, NEG_INF)
        attn = jax.nn.softmax(logits, axis=-1)
        out = jnp.einsum('bhqk,bkhd->bqhd', attn, v).reshape(bs, n, EMBED_DIM)
        out = out @ Wo + bo
        return jax.nn.relu(out)

    def _L1_gnn_ref(graph_input, adj, W, a1, a2):
        import jax, jax.numpy as jnp
        import numpy as np
        ALPHA = 0.2
        NEG_INF = -1000000000.0
        h = jnp.einsum('bnf,of->bno', graph_input, W)
        f1 = h @ a1
        f2 = h @ a2
        e = f1 + jnp.swapaxes(f2, 1, 2)
        e = jax.nn.leaky_relu(e, negative_slope=ALPHA)
        scores = jnp.where(adj == 0, NEG_INF, e)
        attn = jax.nn.softmax(scores, axis=2)
        h_prime = jnp.einsum('bnm,bmf->bnf', attn, graph_input)
        return jax.nn.elu(h_prime)
    x = _layernorm(x + _L0_gnn_ref(x, adj, L0_gnn_Wq, L0_gnn_bq, L0_gnn_Wk, L0_gnn_bk, L0_gnn_Wv, L0_gnn_bv, L0_gnn_Wo, L0_gnn_bo), axis=-1)
    x = _layernorm(x + _L1_gnn_ref(x, adj, L1_gnn_W, L1_gnn_a1, L1_gnn_a2), axis=-1)
    return x

_drawn_inputs = setup_inputs


def setup_inputs(seed=0):
    import zlib

    import numpy as np

    out = dict(_drawn_inputs(seed))
    spreads = {'L0_gnn_bq': (0.0, 0.289),
     'L0_gnn_bk': (0.0, 0.8),
     'L0_gnn_bv': (0.0, 0.1),
     'L0_gnn_bo': (0.0, 0.1)}
    factors = {}
    for name, (base, spread) in spreads.items():
        noise = np.random.default_rng([zlib.crc32(name.encode()), seed]).standard_normal(out[name].shape)
        drawn = base * np.exp(spread * noise) if base else spread * noise
        out[name] = jnp.asarray(drawn.astype(out[name].dtype))
    for name, factor in factors.items():
        out[name] = (out[name] * factor).astype(out[name].dtype)
    return out
```

```python
from contextlib import ExitStack

import concourse.bass as bass
from concourse import mybir

ALU = mybir.AluOpType
ACT = mybir.ActivationFunctionType
AX_X = mybir.AxisListType.X
F32 = mybir.dt.float32
F32R = mybir.dt.float32r
BF16 = mybir.dt.bfloat16
I8 = mybir.dt.int8
I32 = mybir.dt.int32

NEG = -(2.0 ** 100)
EPS = 1e-5
ALPHA = 0.2
P = 128


class Step:

    def __init__(self, b, batches, known):
        at = b if known is None else known
        self.b = b
        self.par = at % 2
        self.next = 0 <= at + 1 < batches
        self.here = 0 <= at < batches
        self.layer1 = 0 <= at - 1 < batches
        self.layer2 = 0 <= at - 2 < batches
        self.after_next = at + 2 < batches


def steps(eng, batches, body):
    first, last = 2, 2 + (batches - 3) // 2 * 2
    for b in range(-1, first):
        body(Step(b, batches, None))
    with eng.Fori(first, last - 1, 2) as b:
        body(Step(b, batches, first))
        body(Step(b + 1, batches, first + 1))
    for b in range(last, batches + 2):
        body(Step(b, batches, None))


def build_program(nc, x, xT, adj, adjT, Wq, bq, Wk, bk, Wv, bv, Wo, bo, W1, a1, a2, out):
    B, N, D = x.shape
    H = 8
    HD = D // H
    NT = N // P
    FT = D // P
    G = FT
    HG = H // G
    UNITS = G * NT
    SCALE = float(HD) ** -0.5

    with ExitStack() as ctx:
        def sb(name, shape, dt=F32):
            return ctx.enter_context(nc.sbuf_tensor(name, shape, dt))

        def ps(name, shape, dt=F32):
            return ctx.enter_context(nc.psum_tensor(name, shape, dt))

        def sem(name):
            return ctx.enter_context(nc.semaphore(name))

        score_bank = [ps(f"score_bank{i}", [P, N]) for i in range(2)]
        a_bank = [ps(f"a_bank{i}", [P, N]) for i in range(2)]
        o_bank = [ps(f"o_bank{g}", [P, N]) for g in range(2)]
        m_bank = [ps(f"m_bank{i}", [P, N]) for i in range(2)]

        ident = sb("ident", [P, P])
        ident_bf = sb("ident_bf", [P, P], BF16)
        ones = sb("ones", [P, P])
        ones_r = sb("ones_r", [2, P], F32R)
        minus_half = sb("minus_half", [P, NT])
        wq_h, wq_l = sb("wq_h", [P, FT, D], F32R), sb("wq_l", [P, FT, D], F32R)
        wk_h, wk_l = sb("wk_h", [P, FT, D], F32R), sb("wk_l", [P, FT, D], F32R)
        wv_h, wv_l = sb("wv_h", [P, FT, D], F32R), sb("wv_l", [P, FT, D], F32R)
        wo = sb("wo", [P, FT, D])
        bq_col, bk_col = sb("bq_col", [P, FT]), sb("bk_col", [P, FT])
        bias_rows = sb("bias_rows", [2, 2, D], F32R)
        a_col = sb("a_col", [P, 2, FT])
        w12 = sb("w12", [P, 2, D])

        xT_in = sb("xT_in", [P, FT, N])
        xT_h, xT_l = sb("xT_h", [P, FT, N], F32R), sb("xT_l", [P, FT, N], F32R)
        q_h, q_l = sb("q_h", [P, N], F32R), sb("q_l", [P, N], F32R)
        k_h, k_l = sb("k_h", [P, N], F32R), sb("k_l", [P, N], F32R)
        KR = 3 * HD + 2
        q_st = [sb(f"q_st{i}", [P, H, N], F32R) for i in range(2)]
        k_st = [sb(f"k_st{i}", [P, H, N], F32R) for i in range(2)]
        v = [sb(f"v{i}", [P, NT, D]) for i in range(2)]
        adj_in = sb("adj_in", [P, NT, N], I32)
        sign = [sb(f"sign{i}", [P, NT, N], I8) for i in range(2)]
        mask_a = [sb(f"mask_a{i}", [P, NT, N], BF16) for i in range(2)]
        mask_t = [sb(f"mask_t{i}", [P, NT, N], BF16) for i in range(2)]
        mask_g = sb("mask_g", [P, NT, N], BF16)
        maxes = sb("maxes", [P, NT, H])
        m_parts = sb("m_parts", [32 + HG, N], F32R)
        m_h, m_l = m_parts[0:HG, :], m_parts[32:32 + HG, :]
        probs = [sb(f"probs{i}", [P, HG, N]) for i in range(2)]
        psums = sb("psums", [P, HG, N])
        oT = sb("oT", [P, G, N])
        y = sb("y", [P, NT, D])
        x1 = sb("x1", [P, NT, D])
        stats1, stats2 = sb("stats1", [P, NT, 6]), sb("stats2", [P, NT, 6])
        mv1, mv2 = sb("mv1", [P, NT, 2]), sb("mv2", [P, NT, 2])
        ve1, ve2 = sb("ve1", [P, NT]), sb("ve2", [P, NT])
        rstd1, rstd2 = sb("rstd1", [P, NT]), sb("rstd2", [P, NT])
        nmean1, nmean2 = sb("nmean1", [P, NT]), sb("nmean2", [P, NT])
        shift1, shift2 = sb("shift1", [P, NT]), sb("shift2", [P, NT])
        f_col = sb("f_col", [P, 2, NT])
        f2_diag = sb("f2_diag", [P, NT, P])
        g_p = sb("g_p", [P, NT, N])
        g_pT = sb("g_pT", [P, NT, N])
        g_max, g_nmax = sb("g_max", [P, NT]), sb("g_nmax", [P, NT])
        g_sum, g_recip = sb("g_sum", [P, NT]), sb("g_recip", [P, NT])
        h1 = sb("h1", [P, NT, D])
        h1e = sb("h1e", [P, 2, D])

        brow = y[0:1, 0:2, :]
        brow_h, brow_l = q_h[0:1, :], q_l[0:1, :]

        d_w, d_rows = sem("d_w"), sem("d_rows")
        d_xT, d_x, d_adj, d_adjT = sem("d_xT"), sem("d_x"), sem("d_adj"), sem("d_adjT")
        d_qst, d_kst, d_mrow, d_out = sem("d_qst"), sem("d_kst"), sem("d_mrow"), sem("d_out")
        c_pool, c_ident, c_dve, c_w12, c_w12sb = (sem("c_pool"), sem("c_ident"), sem("c_dve"), sem("c_w12"),
                                                  sem("c_w12sb"))
        qk_ready, v_ready = sem("qk_ready"), sem("v_ready")
        sa_ready, mT_ready, sb_ready = sem("sa_ready"), sem("mT_ready"), sem("sb_ready")
        pv_done, den_ready, wo_ready, f2_ready = sem("pv_done"), sem("den_ready"), sem("wo_ready"), sem("f2_ready")
        pT_ready, av_ready = sem("pT_ready"), sem("av_ready")
        xh_done, qkh_done, v_done = sem("xh_done"), sem("qkh_done"), sem("v_done")
        exp_done, mh_done = sem("exp_done"), sem("mh_done")
        gadd_done, gexp_done, pT_done, h_done, he_done = (sem("gadd_done"), sem("gexp_done"), sem("pT_done"),
                                                           sem("h_done"), sem("he_done"))
        qkl_done, sign_done, maska_done, maskg_done = (sem("qkl_done"), sem("sign_done"), sem("maska_done"),
                                                       sem("maskg_done"))
        max_done, ml_done, recip_done, o_done = sem("max_done"), sem("ml_done"), sem("recip_done"), sem("o_done")
        y_done, st1_done, mv1_done, x1_done = sem("y_done"), sem("st1_done"), sem("mv1_done"), sem("x1_done")
        leaky_done = sem("leaky_done")
        f_done, diag_done, gmax_done, gnmax_done, grecip_done = (sem("f_done"), sem("diag_done"), sem("gmax_done"),
                                                                 sem("gnmax_done"), sem("grecip_done"))
        z_done, y2_done, st2_done, mv2_done, outn_done = (sem("z_done"), sem("y2_done"), sem("st2_done"),
                                                          sem("mv2_done"), sem("outn_done"))
        xl_done, maskt_done, add_done = sem("xl_done"), sem("maskt_done"), sem("add_done")
        ve1_done, rstd1_done, hneg_done, ve2_done, rstd2_done = (sem("ve1_done"), sem("rstd1_done"),
                                                                 sem("hneg_done"), sem("ve2_done"),
                                                                 sem("rstd2_done"))

        held_dve, held_pool = sem("held_dve"), sem("held_pool")

        ADDS = 3 * H
        W_DMAS = 11

        def due(value):
            return not isinstance(value, int) or value > 0

        def hold(eng, spare):
            eng.sem_inc(spare, 1)

        block = ctx.enter_context(nc.Block())

        @block.sync
        def _(sp):
            sp.dma_start(g_p[:, 0, :].rearrange("p (c o) -> p c o", c=FT),
                         Wq.rearrange("(c p) o -> p c o", p=P)).then_inc(d_w, 16)
            sp.dma_start(g_p[:, 1, :].rearrange("p (c o) -> p c o", c=FT),
                         Wk.rearrange("(c p) o -> p c o", p=P)).then_inc(d_w, 16)
            sp.dma_start(g_p[:, 2, :].rearrange("p (c o) -> p c o", c=FT),
                         Wv.rearrange("(c p) o -> p c o", p=P)).then_inc(d_w, 16)
            sp.dma_start(g_p[:, 3, :].rearrange("p (c o) -> p c o", c=FT),
                         W1.rearrange("(c p) o -> p c o", p=P)).then_inc(d_w, 16)
            sp.dma_start(wo[:], Wo.rearrange("(c p) o -> p c o", p=P)).then_inc(d_w, 16)
            for col, vec in ((bq_col, bq), (bk_col, bk)):
                sp.dma_start(col[:], vec).then_inc(d_w, 16)
            sp.dma_start(a_col[:, 0, :], a1).then_inc(d_w, 16)
            sp.dma_start(a_col[:, 1, :], a2).then_inc(d_w, 16)
            sp.dma_start(brow[:, 0, :], bv.rearrange("(a d) -> a d", a=1)).then_inc(d_w, 16)
            sp.dma_start(brow[:, 1, :], bo.rearrange("(a d) -> a d", a=1)).then_inc(d_w, 16)
            sp.dma_start(xT_in[:], xT[0].rearrange("(c p) n -> p c n", p=P)).then_inc(d_xT, 16)
            sp.dma_start(adj_in[:], adj[0].rearrange("(t p) m -> p t m", p=P)).then_inc(d_adj, 16)
            sp.wait_ge(c_dve, 8)
            sp.dma_start(bias_rows[0:1, :, :].rearrange("p k d -> p (k d)").bitcast(F32), brow_h.bitcast(F32)).then_inc(d_rows, 16)
            sp.dma_start(bias_rows[1:2, :, :].rearrange("p k d -> p (k d)").bitcast(F32), brow_l.bitcast(F32)).then_inc(d_rows, 16)

            def body(s):
                b = s.b
                qs, ks = q_st[1 - s.par], k_st[1 - s.par]

                def stack(g):
                    mine = slice(g * HG, (g + 1) * HG)
                    sp.wait_ge(qkl_done, (b + 1) * 2 * G + 2 * g + 1)
                    sp.dma_start(qs[0:HD, mine, :].bitcast(F32), q_h[:].bitcast(F32)).then_inc(d_qst, 16)
                    sp.dma_start(qs[HD:2 * HD, mine, :].bitcast(F32), q_l[:].bitcast(F32)).then_inc(d_qst, 16)
                    sp.dma_start(qs[2 * HD:3 * HD, mine, :].bitcast(F32), q_h[:].bitcast(F32)).then_inc(d_qst, 16)
                    sp.wait_ge(qkl_done, (b + 1) * 2 * G + 2 * g + 2)
                    sp.dma_start(ks[0:HD, mine, :].bitcast(F32), k_h[:].bitcast(F32)).then_inc(d_kst, 16)
                    sp.dma_start(ks[HD:2 * HD, mine, :].bitcast(F32), k_h[:].bitcast(F32)).then_inc(d_kst, 16)
                    sp.dma_start(ks[2 * HD:3 * HD, mine, :].bitcast(F32), k_l[:].bitcast(F32)).then_inc(d_kst, 16)

                if s.after_next:
                    sp.wait_ge(xh_done, b + 1 + 1)
                    sp.wait_ge(xl_done, b + 1 + 1)
                    sp.dma_start(xT_in[:], xT[b + 2].rearrange("(c p) n -> p c n", p=P)).then_inc(d_xT, 16)
                if s.layer1:
                    if due((b - 2) * NT + NT):
                        sp.wait_ge(x1_done, (b - 2) * NT + NT)
                    sp.dma_start(y[:], x[b - 1].rearrange("(t p) d -> p t d", p=P)).then_inc(d_x, 16)
                if s.next:
                    if due((b - 1) * H * NT + H * NT):
                        sp.wait_ge(sb_ready, (b - 1) * H * NT + H * NT)
                    stack(0)
                    sp.wait_ge(sign_done, b + 1 + 1)
                    sp.dma_start(adj_in[:], adjT[b + 1].rearrange("(t p) m -> p t m", p=P)).then_inc(d_adjT, 16)
                if s.here:
                    sp.wait_ge(ml_done, b * G + 2)
                    sp.dma_start(q_st[s.par][3 * HD:3 * HD + 1, HG:H, :].bitcast(F32),
                                 m_h[:].bitcast(F32)).then_inc(d_mrow, 16)
                    sp.dma_start(q_st[s.par][3 * HD + 1:KR, HG:H, :].bitcast(F32),
                                 m_l[:].bitcast(F32)).then_inc(d_mrow, 16)
                if s.next:
                    stack(1)
                if s.after_next:
                    sp.wait_ge(maskt_done, b + 1 + 1)
                    sp.dma_start(adj_in[:], adj[b + 2].rearrange("(t p) m -> p t m", p=P)).then_inc(d_adj, 16)
                if s.layer2:
                    sp.wait_ge(outn_done, (b - 2) * NT + NT)
                    sp.dma_start(out[b - 2].rearrange("(t p) d -> p t d", p=P), h1[:]).then_inc(d_out, 16)
                if s.next:
                    sp.wait_ge(ml_done, (b + 1) * G + 1)
                    sp.dma_start(qs[3 * HD:3 * HD + 1, 0:HG, :].bitcast(F32), m_h[:].bitcast(F32)).then_inc(d_mrow, 16)
                    sp.dma_start(qs[3 * HD + 1:KR, 0:HG, :].bitcast(F32), m_l[:].bitcast(F32)).then_inc(d_mrow, 16)

            steps(sp, B, body)
            sp.wait_ge(d_out, 16 * B)

        @block.gpsimd
        def _(pool):
            pool.memset(ones[:], 1.0).then_inc(c_pool, 1)
            pool.memset(minus_half[:], -0.5).then_inc(c_pool, 1)
            pool.wait_ge(c_pool, 1)
            pool.affine_select(out=ident[:], in_=ones[:], compare_op=ALU.is_equal, fill=0.0, base=0,
                               pattern=[[-1, P]], channel_multiplier=1).then_inc(c_ident, 1)

            def split_xT(batch):
                pool.wait_ge(xh_done, batch + 1)
                if due((batch - 1) * 2 * G + 2 * G):
                    pool.wait_ge(qk_ready, (batch - 1) * 2 * G + 2 * G)
                pool.tensor_tensor(xT_l[:], xT_in[:], xT_h[:].bitcast(F32), ALU.subtract).then_inc(xl_done, 1)

            split_xT(0)

            def body(s):
                b = s.b

                def add_keys(u):
                    g, t = divmod(u, NT)
                    if t == 0:
                        return
                    for j in range(HG):
                        pool.wait_ge(exp_done, b * H * NT + HG * u + j + 1)
                        n = g * 3 * HG + (t - 1) * HG + j
                        if t == 1:
                            if j == 0:
                                if due(b * G + g):
                                    pool.wait_ge(den_ready, b * G + g)
                            pool.tensor_tensor(psums[:, j, :], probs[(u - 1) % 2][:, j, :],
                                               probs[u % 2][:, j, :], ALU.add).then_inc(add_done, 1)
                        else:
                            pool.wait_ge(add_done, b * ADDS + n - HG + 1)
                            pool.tensor_tensor(psums[:, j, :], psums[:, j, :],
                                               probs[u % 2][:, j, :], ALU.add).then_inc(add_done, 1)

                def negative_part(i):
                    if not s.layer2:
                        return
                    pool.wait_ge(h_done, (b - 2) * NT + 2 * i + 2)
                    if i == 1:
                        pool.wait_ge(z_done, (b - 2) * 2 + 1)
                    hold(pool, held_pool)
                    pool.tensor_scalar(h1e[:], h1[:, 2 * i:2 * i + 2, :], 0.0, -3.0e38,
                                       ALU.min, ALU.max).then_inc(hneg_done, 1)

                if s.here:
                    add_keys(1)
                    add_keys(2)
                negative_part(0)
                if s.here:
                    add_keys(3)
                negative_part(1)
                if s.layer1:
                    pool.wait_ge(mv1_done, (b - 1) * NT + NT)
                    hold(pool, held_pool)
                    pool.tensor_scalar(ve1[:], mv1[:, :, 1], EPS, 1.0, ALU.add, ALU.mult).then_inc(ve1_done, 1)
                    pool.tensor_scalar(nmean1[:], mv1[:, :, 0], -1.0, 1.0, ALU.mult, ALU.mult).then_inc(ve1_done, 1)
                    pool.wait_ge(ve1_done, (b - 1) * 2 + 2)
                    pool.tensor_tensor(rstd1[:], ve1[:], minus_half[:], ALU.pow).then_inc(rstd1_done, 1)
                    pool.wait_ge(rstd1_done, (b - 1) * 2 + 1)
                    pool.tensor_tensor(shift1[:], nmean1[:], rstd1[:], ALU.mult).then_inc(rstd1_done, 1)
                if s.here:
                    add_keys(5)
                if s.layer2:
                    pool.wait_ge(mv2_done, (b - 2) * NT + NT)
                    hold(pool, held_pool)
                    pool.tensor_scalar(ve2[:], mv2[:, :, 1], EPS, 1.0, ALU.add, ALU.mult).then_inc(ve2_done, 1)
                    pool.tensor_scalar(nmean2[:], mv2[:, :, 0], -1.0, 1.0, ALU.mult, ALU.mult).then_inc(ve2_done, 1)
                    pool.wait_ge(ve2_done, (b - 2) * 2 + 2)
                    pool.tensor_tensor(rstd2[:], ve2[:], minus_half[:], ALU.pow).then_inc(rstd2_done, 1)
                    pool.wait_ge(rstd2_done, (b - 2) * 2 + 1)
                    pool.tensor_tensor(shift2[:], nmean2[:], rstd2[:], ALU.mult).then_inc(rstd2_done, 1)
                if s.here:
                    add_keys(6)
                if s.after_next:
                    split_xT(b + 2)
                if s.here:
                    add_keys(7)

            steps(pool, B, body)

        @block.scalar
        def _(act):
            def split_xT(batch):
                act.wait_ge(d_xT, batch * 16 + 16)
                if due((batch - 1) * 2 * G + 2 * G):
                    act.wait_ge(qk_ready, (batch - 1) * 2 * G + 2 * G)
                act.copy(xT_h[:], xT_in[:]).then_inc(xh_done, 1)

            split_xT(0)

            def body(s):
                b = s.b

                def exp_chunk(u, j):
                    c = HG * u + j
                    if not s.here:
                        return
                    act.wait_ge(sb_ready, b * H * NT + c + 1)
                    if due(b * UNITS + u - 1):
                        act.wait_ge(pv_done, b * UNITS + u - 1)
                    g, t = divmod(u, NT)
                    before = {0: g * 3 * HG - HG + j + 1 if g else -HG + j + 1,
                              1: g * 3 * HG,
                              2: g * 3 * HG + j + 1,
                              3: g * 3 * HG + HG + j + 1}[t]
                    if due(b * ADDS + before):
                        act.wait_ge(add_done, b * ADDS + before)
                    act.activation(probs[u % 2][:, j, :], score_bank[c % 2][:], ACT.Exp,
                                   scale=SCALE).then_inc(exp_done, 1)

                def high_part(i):
                    if not s.next:
                        return
                    g = i // 2
                    dst, col, d_st = ((q_h, bq_col, d_qst), (k_h, bk_col, d_kst))[i % 2]
                    bank = m_bank[(0, 1, 1, 0)[i]]
                    act.wait_ge(qk_ready, (b + 1) * 2 * G + i + 1)
                    if due((b + 1) * 3 * 16 * G + 3 * 16 * g):
                        act.wait_ge(d_st, (b + 1) * 3 * 16 * G + 3 * 16 * g)
                    if due((b + 1) * 2 * G + i - 1):
                        act.wait_ge(qkl_done, (b + 1) * 2 * G + i - 1)
                    act.activation(dst[:], bank[:], ACT.Identity,
                                   bias=col[:, g:g + 1]).then_inc(qkh_done, 1)

                def evacuate_pT(t):
                    if not s.layer2:
                        return
                    act.wait_ge(pT_ready, (b - 2) * NT + t + 1)
                    act.copy(g_pT[:, t, :], m_bank[t % 2][:]).then_inc(pT_done, 1)

                def high_max(batch, g):
                    act.wait_ge(mT_ready, batch * G + g + 1)
                    if due(batch * 2 * 16 * G + 2 * 16 * g):
                        act.wait_ge(d_mrow, batch * 2 * 16 * G + 2 * 16 * g)
                    if due(batch * G + g):
                        act.wait_ge(ml_done, batch * G + g)
                    act.activation(m_h[:], m_bank[1][0:HG, :], ACT.Copy, scale=-1.0).then_inc(mh_done, 1)

                def take_v(i):
                    if not s.next:
                        return
                    act.wait_ge(v_ready, (b + 1) * 2 + i + 1)
                    if due((b - 1) * UNITS + UNITS):
                        act.wait_ge(pv_done, (b - 1) * UNITS + UNITS)
                    act.copy(v[1 - s.par][:, 2 * i:2 * i + 2, :],
                             m_bank[1 - i][:].rearrange("p (t d) -> p t d", t=2)).then_inc(v_done, 1)

                def divide(i):
                    if not s.layer2:
                        return
                    act.wait_ge(grecip_done, b - 2 + 1)
                    act.wait_ge(av_ready, (b - 2) * 2 + i + 1)
                    for t in (2 * i, 2 * i + 1):
                        act.activation(h1[:, t, :], m_bank[1 - i][:, (t % 2) * D:(t % 2 + 1) * D], ACT.Copy,
                                       scale=g_recip[:, t:t + 1]).then_inc(h_done, 1)

                def exp_negative(i):
                    if not s.layer2:
                        return
                    act.wait_ge(hneg_done, (b - 2) * 2 + i + 1)
                    act.activation(h1e[:], h1e[:], ACT.Exp).then_inc(he_done, 1)

                def normalise1():
                    if not s.layer1:
                        return
                    act.wait_ge(rstd1_done, (b - 1) * 2 + 2)
                    if due((b - 2) * 2 + 2):
                        act.wait_ge(y2_done, (b - 2) * 2 + 2)
                    for t in range(NT):
                        act.activation(x1[:, t, :], y[:, t, :], ACT.Identity, scale=rstd1[:, t:t + 1],
                                       bias=shift1[:, t:t + 1]).then_inc(x1_done, 1)

                def normalise2():
                    if not s.layer2:
                        return
                    act.wait_ge(rstd2_done, (b - 2) * 2 + 2)
                    for t in range(NT):
                        act.activation(h1[:, t, :], h1[:, t, :], ACT.Identity, scale=rstd2[:, t:t + 1],
                                       bias=shift2[:, t:t + 1]).then_inc(outn_done, 1)

                for u in range(UNITS):
                    exp_chunk(u, 0)
                    exp_chunk(u, 1)
                    if u == 0:
                        high_part(0)
                    if u == 5:
                        normalise1()
                    if u == 6:
                        normalise2()
                    if u == 2:
                        divide(0)
                    if u == 3 and s.here:
                        high_max(b, 1)
                    if u == 3:
                        divide(1)
                    if u == 7 and s.next:
                        high_max(b + 1, 0)
                    exp_chunk(u, 2)
                    exp_chunk(u, 3)
                    if u == 0:
                        high_part(1)
                    if u < 2:
                        evacuate_pT(2 * u)
                        evacuate_pT(2 * u + 1)
                    if u == 2:
                        take_v(0)
                    if u == 3:
                        exp_negative(0)
                    if u == 4:
                        take_v(1)
                        exp_negative(1)
                        high_part(2)
                    if u == 5:
                        high_part(3)
                    if u == 6 and s.after_next:
                        split_xT(b + 2)
                    if u == 7 and s.layer1:
                        for t in range(NT):
                            act.wait_ge(gmax_done, (b - 1) * NT + t + 1)
                            act.activation(g_p[:, t, :], g_p[:, t, :], ACT.Identity,
                                           bias=f_col[:, 0, t:t + 1]).then_inc(gadd_done, 1)
                        act.wait_ge(gnmax_done, (b - 1) * 3 + 3)
                        for t in range(NT):
                            act.wait_ge(leaky_done, (b - 1) * NT + t + 1)
                            act.activation(g_p[:, t, :], g_p[:, t, :], ACT.Exp, bias=g_nmax[:, t:t + 1],
                                           accum_out=g_sum[:, t:t + 1]).then_inc(gexp_done, 1)
                    if u == 7 and s.layer2:
                        act.wait_ge(d_out, (b - 2) * 16 + 16)

            steps(act, B, body)

        @block.vector
        def _(dve):
            dve.memset(ones_r[:].bitcast(F32), 1.0)
            dve.memset(k_st[0][3 * HD:KR, :, :].bitcast(F32), 1.0)
            dve.memset(k_st[1][3 * HD:KR, :, :].bitcast(F32), 1.0)
            dve.wait_ge(c_ident, 1)
            dve.tensor_copy(ident_bf[:], ident[:])
            dve.wait_ge(d_w, 16 * W_DMAS)
            pairs = []
            for n, (hi, lo) in enumerate(((wq_h, wq_l), (wk_h, wk_l), (wv_h, wv_l))):
                for c in range(FT):
                    src = g_p[:, n, c * D:(c + 1) * D]
                    if n < 2:
                        src = src.rearrange("p (g j d) -> p g d j", g=G, j=HG)
                        pairs.append((hi[:, c, :].rearrange("p (g d j) -> p g d j", g=G, j=HG),
                                      lo[:, c, :].rearrange("p (g d j) -> p g d j", g=G, j=HG), src))
                    else:
                        pairs.append((hi[:, c, :], lo[:, c, :], src))
            for hi, lo, src in pairs:
                dve.tensor_copy(hi, src)
            browf = brow.rearrange("p k d -> p (k d)")
            dve.tensor_copy(brow_h, browf).then_inc(c_dve, 1)
            dve.wait_ge(c_dve, 1)
            for hi, lo, src in pairs:
                dve.tensor_tensor(lo, src, hi.bitcast(F32), ALU.subtract).then_inc(c_dve, 1)
            dve.tensor_tensor(brow_l, browf, brow_h.bitcast(F32), ALU.subtract).then_inc(c_dve, 1)
            for k in range(2):
                for c in range(FT):
                    dve.tensor_scalar(f2_diag[:, 2 * k + c, :], ones[:], a_col[:, k, c:c + 1], None,
                                      ALU.mult).then_inc(c_dve, 1)
            dve.wait_ge(c_w12, 1)
            dve.tensor_copy(w12[:], m_bank[0][:].rearrange("p (k d) -> p k d", k=2)).then_inc(c_w12sb, 1)
            dve.wait_ge(c_w12sb, 1)

            def body(s):
                b = s.b

                def low_part(i):
                    g = i // 2
                    hi, lo, col, d_st = ((q_h, q_l, bq_col, d_qst), (k_h, k_l, bk_col, d_kst))[i % 2]
                    dve.wait_ge(qkh_done, (b + 1) * 2 * G + i + 1)
                    if due((b + 1) * 3 * 16 * G + 3 * 16 * g):
                        dve.wait_ge(d_st, (b + 1) * 3 * 16 * G + 3 * 16 * g)
                    dve.scalar_tensor_tensor(out=lo[:], in0=m_bank[(0, 1, 1, 0)[i]][:], scalar=col[:, g:g + 1],
                                             in1=hi[:].bitcast(F32), op0=ALU.add,
                                             op1=ALU.subtract).then_inc(qkl_done, 1)

                def maxima(batch, first, last):
                    for n in range(first, last):
                        h, t = divmod(n, NT)
                        dve.wait_ge(sa_ready, batch * H * NT + n + 1)
                        hold(dve, held_dve)
                        dve.tensor_tensor_reduce(a_bank[n % 2][:], a_bank[n % 2][:],
                                                 mask_a[s.par if first >= 20 else 1 - s.par][:, t, :], 1.0, -3.0e38,
                                                 ALU.add, ALU.max, maxes[:, t, h:h + 1]).then_inc(max_done, 1)

                def pair(u, i):
                    n = 4 * u + 2 * i
                    if u < 3:
                        if s.here:
                            maxima(b, 20 + n, 22 + n)
                    elif s.next:
                        maxima(b + 1, n - 12, n - 10)

                def normalised(batch, g):
                    dve.wait_ge(den_ready, batch * G + g + 1)
                    if due((batch - 1) * 2 + 2):
                        dve.wait_ge(wo_ready, (batch - 1) * 2 + 2)
                    dve.reciprocal(oT[:, g, :], m_bank[1 - g][:]).then_inc(recip_done, 1)
                    dve.wait_ge(recip_done, batch * G + g + 1)
                    dve.wait_ge(pv_done, batch * UNITS + (g + 1) * NT)
                    dve.tensor_tensor(oT[:, g, :], o_bank[g][:], oT[:, g, :], ALU.mult).then_inc(o_done, 1)

                def low_max(batch, g):
                    dve.wait_ge(mh_done, batch * G + g + 1)
                    if due(batch * 2 * 16 * G + 2 * 16 * g):
                        dve.wait_ge(d_mrow, batch * 2 * 16 * G + 2 * 16 * g)
                    dve.scalar_tensor_tensor(out=m_l[:], in0=m_bank[1][0:HG, :], scalar=-1.0,
                                             in1=m_h[:].bitcast(F32), op0=ALU.mult,
                                             op1=ALU.subtract).then_inc(ml_done, 1)

                def residual(i):
                    if not s.layer1:
                        return
                    dve.wait_ge(d_x, (b - 1) * 16 + 16)
                    dve.wait_ge(wo_ready, (b - 1) * 2 + i + 1)
                    dve.scalar_tensor_tensor(
                        out=y[:, 2 * i:2 * i + 2, :], in0=m_bank[1 - i][:].rearrange("p (t d) -> p t d", t=2),
                        scalar=0.0, in1=y[:, 2 * i:2 * i + 2, :], op0=ALU.max, op1=ALU.add).then_inc(y_done, 1)

                def elu(i):
                    if not s.layer2:
                        return
                    half = slice(2 * i, 2 * i + 2)
                    dve.wait_ge(he_done, (b - 2) * 2 + i + 1)
                    dve.wait_ge(av_ready, (b - 2) * 2 + 2)
                    dve.scalar_tensor_tensor(out=x1[:, half, :], in0=h1e[:], scalar=-1.0, in1=x1[:, half, :],
                                             op0=ALU.add, op1=ALU.add).then_inc(z_done, 1)
                    dve.wait_ge(z_done, (b - 2) * 2 + i + 1)
                    dve.scalar_tensor_tensor(out=h1[:, half, :], in0=h1[:, half, :], scalar=0.0,
                                             in1=x1[:, half, :], op0=ALU.max, op1=ALU.add).then_inc(y2_done, 1)

                pair(0, 0)
                if s.next:
                    low_part(0)
                pair(0, 1)
                if s.next:
                    low_part(1)
                if s.layer2:
                    dve.wait_ge(gexp_done, (b - 2) * NT + NT)
                    dve.reciprocal(g_recip[:], g_sum[:]).then_inc(grecip_done, 1)
                pair(1, 0)
                if s.layer1:
                    dve.tensor_scalar(mask_g[:], sign[1 - s.par][:], 0.0, NEG,
                                      ALU.is_equal, ALU.mult).then_inc(maskg_done, 1)
                if s.next:
                    dve.wait_ge(d_adj, (b + 1) * 16 + 16)
                    if due(b):
                        dve.wait_ge(maskg_done, b)
                    dve.tensor_scalar(sign[1 - s.par][:], adj_in[:], 1.0, -1.0,
                                      ALU.min, ALU.max).then_inc(sign_done, 1)
                pair(1, 1)
                if s.layer1:
                    normalised(b - 1, 1)
                pair(2, 0)
                if s.next:
                    dve.wait_ge(sign_done, b + 1 + 1)
                    dve.tensor_scalar(mask_a[1 - s.par][:], sign[1 - s.par][:], 0.0, NEG,
                                      ALU.is_le, ALU.mult).then_inc(maska_done, 1)
                pair(2, 1)
                if s.next:
                    dve.wait_ge(maska_done, b + 1 + 1)
                pair(3, 0)
                if s.here:
                    low_max(b, 1)
                pair(3, 1)
                if s.next:
                    dve.wait_ge(d_adjT, (b + 1) * 16 + 16)
                    if due((b - 1) * H * NT + H * NT):
                        dve.wait_ge(sb_ready, (b - 1) * H * NT + H * NT)
                    dve.tensor_scalar(mask_t[1 - s.par][:], adj_in[:], 0.0, NEG,
                                      ALU.is_le, ALU.mult).then_inc(maskt_done, 1)
                residual(0)
                residual(1)
                pair(4, 0)
                if s.layer1:
                    dve.wait_ge(y_done, (b - 1) * 2 + 2)
                    for t in range(NT):
                        dve.bn_stats(stats1[:, t, :], y[:, t, :]).then_inc(st1_done, 1)
                    dve.wait_ge(st1_done, (b - 1) * NT + NT)
                    hold(dve, held_dve)
                    for t in range(NT):
                        dve.bn_aggr(mv1[:, t, :], stats1[:, t, :]).then_inc(mv1_done, 1)
                elu(0)
                pair(4, 1)
                if s.next:
                    low_part(2)
                elu(1)
                pair(5, 0)
                if s.layer2:
                    dve.wait_ge(y2_done, (b - 2) * 2 + 2)
                    for t in range(NT):
                        dve.bn_stats(stats2[:, t, :], h1[:, t, :]).then_inc(st2_done, 1)
                    dve.wait_ge(st2_done, (b - 2) * NT + NT)
                    hold(dve, held_dve)
                    for t in range(NT):
                        dve.bn_aggr(mv2[:, t, :], stats2[:, t, :]).then_inc(mv2_done, 1)
                if s.next:
                    low_part(3)
                pair(5, 1)
                if s.layer1:
                    dve.wait_ge(x1_done, (b - 1) * NT + NT)
                    if due(b - 2 + 1):
                        dve.wait_ge(f2_ready, b - 2 + 1)
                    for n in range(2 * NT):
                        k, t = divmod(n, NT)
                        if n >= 2:
                            dve.wait_ge(f_done, (b - 1) * 2 * NT + n - 1)
                        junk = f2_diag[:, 2 * (n % 2):2 * (n % 2) + 2, :].rearrange("p a b -> p (a b)")
                        dve.tensor_tensor_reduce(junk, x1[:, t, :], w12[:, k, :], 1.0, 0.0, ALU.mult, ALU.add,
                                                 f_col[:, k, t:t + 1]).then_inc(f_done, 1)
                    dve.wait_ge(f_done, (b - 1) * 2 * NT + 2 * NT)
                    for t in range(NT):
                        dve.tensor_scalar(f2_diag[:, t, :], ident[:], f_col[:, 1, t:t + 1], None,
                                          ALU.mult).then_inc(diag_done, 1)
                pair(6, 0)
                if s.here:
                    normalised(b, 0)
                pair(6, 1)
                if s.layer1:
                    if due((b - 2) * NT + NT):
                        dve.wait_ge(pT_ready, (b - 2) * NT + NT)
                    dve.wait_ge(f2_ready, b)
                    hold(dve, held_dve)
                    for t in range(NT):
                        dve.tensor_tensor_reduce(g_p[:, t, :], m_bank[0][:], mask_g[:, t, :], 1.0, -3.0e38,
                                                 ALU.add, ALU.max, g_max[:, t:t + 1]).then_inc(gmax_done, 1)
                    dve.wait_ge(gmax_done, (b - 1) * NT + NT)
                    dve.tensor_tensor(g_max[:], g_max[:], f_col[:, 0, :], ALU.add).then_inc(gnmax_done, 1)
                    dve.wait_ge(gnmax_done, (b - 1) * 3 + 1)
                    dve.scalar_tensor_tensor(out=g_nmax[:], in0=g_max[:], scalar=ALPHA, in1=g_max[:],
                                             op0=ALU.mult, op1=ALU.max).then_inc(gnmax_done, 1)
                    dve.wait_ge(gnmax_done, (b - 1) * 3 + 2)
                    dve.tensor_scalar(g_nmax[:], g_nmax[:], -1.0, None, ALU.mult).then_inc(gnmax_done, 1)
                pair(7, 0)
                if s.next:
                    low_max(b + 1, 0)
                pair(7, 1)
                if s.layer1:
                    for t in range(NT):
                        dve.wait_ge(gadd_done, (b - 1) * NT + t + 1)
                        dve.scalar_tensor_tensor(out=g_p[:, t, :], in0=g_p[:, t, :], scalar=ALPHA, in1=g_p[:, t, :],
                                                 op0=ALU.mult, op1=ALU.max).then_inc(leaky_done, 1)

            steps(dve, B, body)

        @block.tensor
        def _(pe):
            pe.wait_ge(d_w, 16 * W_DMAS)
            pe.wait_ge(c_dve, 12)
            for k in range(2):
                for c in range(FT):
                    mm = pe.matmul(m_bank[0][:, k * D:(k + 1) * D], f2_diag[:, 2 * k + c, :],
                                   g_p[:, 3, c * D:(c + 1) * D], start=(c == 0), stop=(c == FT - 1))
            mm.then_inc(c_w12, 1)
            pe.wait_ge(c_w12sb, 1)
            pe.wait_ge(d_rows, 32)

            def body(s):
                b = s.b
                qn, kn = q_st[1 - s.par], k_st[1 - s.par]
                qs, ks = q_st[s.par], k_st[s.par]

                def scores(u, j):
                    if not s.here:
                        return
                    g, t = divmod(u, NT)
                    c, h = HG * u + j, g * HG + j
                    bank = score_bank[c % 2][:]
                    if j == 0:
                        pe.wait_ge(maskt_done, b + 1)
                        pe.wait_ge(d_mrow, b * 2 * 16 * G + 2 * 16 * (g + 1))
                    if due(b * H * NT + c - 1):
                        pe.wait_ge(exp_done, b * H * NT + c - 1)
                    pe.matmul(bank, ident_bf[:], mask_t[s.par][:, t, :], start=True, stop=False)
                    pe.matmul(bank, ks[0:KR, h, t * P:(t + 1) * P], qs[0:KR, h, :],
                              start=False, stop=True).then_inc(sb_ready, 1)

                def weigh(batch, par, u):
                    g, t = divmod(u, NT)
                    if t == 0:
                        pe.wait_ge(v_done, batch * 2 + 2)
                        if due((batch - 1) * G + g + 1):
                            pe.wait_ge(o_done, (batch - 1) * G + g + 1)
                    pe.wait_ge(exp_done, batch * H * NT + HG * (u + 1))
                    for j in range(HG):
                        h = g * HG + j
                        mm = pe.matmul(o_bank[g][HD * j:HD * (j + 1), :], v[par][:, t, h * HD:(h + 1) * HD],
                                       probs[u % 2][:, j, :], start=(t == 0), stop=(t == NT - 1))
                    mm.then_inc(pv_done, 1)

                def project(i):
                    g = i // 2
                    bank = m_bank[(0, 1, 1, 0)[i]][:]
                    wh, wl = ((wq_h, wq_l), (wk_h, wk_l))[i % 2]
                    n = 0
                    for c in range(FT):
                        for w, xx in ((wh, xT_h), (wh, xT_l), (wl, xT_h)):
                            n += 1
                            mm = pe.matmul(bank, w[:, c, g * P:(g + 1) * P], xx[:, c, :],
                                           start=(n == 1), stop=(n == 3 * FT))
                    mm.then_inc(qk_ready, 1)

                def project_v(i):
                    for t in (2 * i, 2 * i + 1):
                        dst = m_bank[1 - i][:, (t % 2) * D:(t % 2 + 1) * D]
                        pe.matmul(dst, ones_r[:], bias_rows[:, 0, :], start=True, stop=False)
                        n = 0
                        for c in range(FT):
                            for xx, w in ((xT_h, wv_h), (xT_l, wv_h), (xT_h, wv_l)):
                                n += 1
                                mm = pe.matmul(dst, xx[:, c, t * P:(t + 1) * P], w[:, c, :],
                                               start=False, stop=(n == 3 * FT))
                    mm.then_inc(v_ready, 1)

                def denominators(batch, g):
                    pe.wait_ge(add_done, batch * ADDS + (g + 1) * 3 * HG)
                    for j in range(HG):
                        mm = pe.matmul(m_bank[1 - g][HD * j:HD * (j + 1), :], ones[:, 0:HD], psums[:, j, :],
                                       start=True, stop=True)
                    mm.then_inc(den_ready, 1)

                def row_scores(batch, first, last):
                    q, k = (qs, ks) if first >= 20 else (qn, kn)
                    for n in range(first, last):
                        h, t = divmod(n, NT)
                        if t == 0 and h % HG == 0:
                            pe.wait_ge(d_qst, batch * 3 * 16 * G + 3 * 16 * (h // HG + 1))
                            pe.wait_ge(d_kst, batch * 3 * 16 * G + 3 * 16 * (h // HG + 1))
                        if due(batch * H * NT + n - 1):
                            pe.wait_ge(max_done, batch * H * NT + n - 1)
                        pe.matmul(a_bank[n % 2][:], q[0:3 * HD, h, t * P:(t + 1) * P], k[0:3 * HD, h, :],
                                  start=True, stop=True).then_inc(sa_ready, 1)

                def pair(u, i):
                    n = 4 * u + 2 * i
                    if u < 3:
                        if s.here:
                            row_scores(b, 20 + n, 22 + n)
                    elif s.next:
                        row_scores(b + 1, n - 12, n - 10)

                def turn_max(batch, g):
                    pe.wait_ge(max_done, batch * H * NT + (g + 1) * HG * NT)
                    for t in range(NT):
                        mm = pe.transpose(m_bank[1][0:HG, t * P:(t + 1) * P],
                                          maxes[:, t, g * HG:(g + 1) * HG], ident[:])
                    mm.then_inc(mT_ready, 1)

                def turn_graph(t):
                    for r in range(NT):
                        mm = pe.transpose(m_bank[t % 2][:, r * P:(r + 1) * P], g_p[:, r, t * P:(t + 1) * P], ident[:])
                    mm.then_inc(pT_ready, 1)

                def graph_sum(i):
                    pe.wait_ge(pT_done, (b - 2) * NT + NT)
                    for r in (2 * i, 2 * i + 1):
                        for t in range(NT):
                            mm = pe.matmul(m_bank[1 - i][:, (r % 2) * D:(r % 2 + 1) * D],
                                           g_pT[:, t, r * P:(r + 1) * P], x1[:, t, :],
                                           start=(t == 0), stop=(t == NT - 1))
                    mm.then_inc(av_ready, 1)

                def output_projection(i):
                    for t in (2 * i, 2 * i + 1):
                        dst = m_bank[1 - i][:, (t % 2) * D:(t % 2 + 1) * D]
                        pe.matmul(dst, ones_r[:], bias_rows[:, 1, :], start=True, stop=False)
                        for g in range(G):
                            mm = pe.matmul(dst, oT[:, g, t * P:(t + 1) * P], wo[:, g, :],
                                           start=False, stop=(g == G - 1))
                    mm.then_inc(wo_ready, 1)

                for u in range(UNITS):
                    scores(u, 0)
                    scores(u, 1)
                    pair(u, 0)
                    if u == 0 and s.next:
                        pe.wait_ge(xh_done, b + 1 + 1)
                        pe.wait_ge(xl_done, b + 1 + 1)
                        if due((b - 2) * NT + NT):
                            pe.wait_ge(gmax_done, (b - 2) * NT + NT)
                        if due(b * 2 * G + 2 * G):
                            pe.wait_ge(qkl_done, b * 2 * G + 2 * G)
                        project(0)
                    if u == 1 and s.layer2:
                        pe.wait_ge(gexp_done, (b - 2) * NT + NT)
                        if s.next:
                            pe.wait_ge(qkl_done, (b + 1) * 2 * G + 1)
                        else:
                            pe.wait_ge(gmax_done, (b - 2) * NT + NT)
                        turn_graph(0)
                        if s.next:
                            pe.wait_ge(qkl_done, (b + 1) * 2 * G + 2)
                        elif s.here:
                            pe.wait_ge(ml_done, b * G + 1)
                        turn_graph(1)
                    if u == 2 and s.next:
                        if s.layer2:
                            pe.wait_ge(h_done, (b - 2) * NT + 2)
                        else:
                            pe.wait_ge(qkl_done, (b + 1) * 2 * G + 2)
                        project_v(0)
                    if u == 3 and s.here:
                        if s.next:
                            pe.wait_ge(v_done, (b + 1) * 2 + 1)
                        else:
                            pe.wait_ge(h_done, (b - 2) * NT + 2)
                        turn_max(b, 1)
                    if u == 4 and s.next:
                        if s.layer1:
                            pe.wait_ge(y_done, (b - 1) * 2 + 2)
                        else:
                            pe.wait_ge(qkl_done, (b + 1) * 2 * G + 1)
                        project_v(1)
                    if u == 5 and s.next:
                        pe.wait_ge(v_done, (b + 1) * 2 + 2)
                        project(3)
                    if u == 6 and s.layer1:
                        pe.wait_ge(diag_done, (b - 1) * NT + NT)
                        if s.next:
                            pe.wait_ge(qkl_done, (b + 1) * 2 * G + 4)
                        pe.matmul(m_bank[0][:], ones[:], f2_diag[:].rearrange("p t n -> p (t n)"),
                                  start=True, stop=True).then_inc(f2_ready, 1)
                    if u == 7 and s.next:
                        if s.here:
                            pe.wait_ge(recip_done, b * G + 1)
                        else:
                            pe.wait_ge(qkl_done, (b + 1) * 2 * G + 3)
                        turn_max(b + 1, 0)
                    scores(u, 2)
                    scores(u, 3)
                    pair(u, 1)
                    if u == 0:
                        if s.layer1:
                            weigh(b - 1, 1 - s.par, UNITS - 1)
                    elif s.here:
                        weigh(b, s.par, u - 1)
                    if u == 0 and s.next:
                        if due(b * G + 1):
                            pe.wait_ge(ml_done, b * G + 1)
                        project(1)
                    if u == 1:
                        if s.layer2:
                            pe.wait_ge(pT_done, (b - 2) * NT + 1)
                            turn_graph(2)
                            pe.wait_ge(pT_done, (b - 2) * NT + 2)
                            turn_graph(3)
                        if s.layer1:
                            if s.layer2:
                                pe.wait_ge(pT_done, (b - 2) * NT + 3)
                            else:
                                pe.wait_ge(qkl_done, (b + 1) * 2 * G + 1)
                            denominators(b - 1, 1)
                        if s.layer2:
                            graph_sum(0)
                    if u == 2 and s.layer2:
                        if s.layer1:
                            pe.wait_ge(recip_done, (b - 1) * G + 2)
                        graph_sum(1)
                    if u == 3 and s.layer1:
                        pe.wait_ge(o_done, (b - 1) * G + G)
                        if s.here:
                            pe.wait_ge(ml_done, b * G + 2)
                        else:
                            pe.wait_ge(h_done, (b - 2) * NT + 2)
                        output_projection(0)
                        if due((b - 2) * NT + NT):
                            pe.wait_ge(h_done, (b - 2) * NT + NT)
                        output_projection(1)
                    if u == 4 and s.next:
                        if s.layer1:
                            pe.wait_ge(y_done, (b - 1) * 2 + 1)
                        elif s.here:
                            pe.wait_ge(ml_done, b * G + 2)
                        else:
                            pe.wait_ge(v_done, (b + 1) * 2 + 1)
                        project(2)
                    if u == 5 and s.here:
                        if s.next:
                            pe.wait_ge(qkl_done, (b + 1) * 2 * G + 3)
                        else:
                            pe.wait_ge(y_done, (b - 1) * 2 + 1)
                        denominators(b, 0)

            steps(pe, B, body)


def kernel(x, adj, L0_gnn_Wq, L0_gnn_bq, L0_gnn_Wk, L0_gnn_bk, L0_gnn_Wv, L0_gnn_bv, L0_gnn_Wo, L0_gnn_bo,
           L1_gnn_W, L1_gnn_a1, L1_gnn_a2):
    import numpy as np
    import concourse.bacc as bacc
    from concourse.bass_utils import run_bass_kernel_spmd

    x, adj = np.asarray(x), np.asarray(adj)

    def by_dim(vec):
        return np.asarray(vec).reshape(2, 4, 32).transpose(2, 1, 0).reshape(128, 2)

    def by_tile(vec):
        return np.asarray(vec).reshape(2, 128).T

    given = {
        "x": x, "xT": x.transpose(0, 2, 1), "adj": adj, "adjT": adj.transpose(0, 2, 1),
        "Wq": L0_gnn_Wq, "bq": by_dim(L0_gnn_bq), "Wk": L0_gnn_Wk, "bk": by_dim(L0_gnn_bk),
        "Wv": L0_gnn_Wv, "bv": L0_gnn_bv, "Wo": L0_gnn_Wo, "bo": L0_gnn_bo,
        "W1": L1_gnn_W, "a1": by_tile(L1_gnn_a1), "a2": by_tile(L1_gnn_a2),
    }
    nc = bacc.Bacc("TRN2", target_bir_lowering=False, num_devices=1)
    arrays, args = {}, []
    for name, value in given.items():
        a = np.ascontiguousarray(value)
        arrays[f"in_{name}"] = a
        args.append(nc.dram_tensor(f"in_{name}", a.shape, mybir.dt.from_np(a.dtype), kind="ExternalInput").ap())
    out = nc.dram_tensor("out_x", x.shape, F32, kind="ExternalOutput").ap()
    build_program(nc, *args, out)
    r = run_bass_kernel_spmd(nc, [arrays], core_ids=[0])
    return r.results[0]["out_x"]
```

```python
from contextlib import ExitStack

import concourse.bass as bass
from concourse import mybir

ALU = mybir.AluOpType
ACT = mybir.ActivationFunctionType
AX_X = mybir.AxisListType.X
F32 = mybir.dt.float32
F32R = mybir.dt.float32r
BF16 = mybir.dt.bfloat16
I8 = mybir.dt.int8
I32 = mybir.dt.int32

NEG = -(2.0 ** 100)
EPS = 1e-5
ALPHA = 0.2
P = 128


class Step:

    def __init__(self, b, batches, known):
        at = b if known is None else known
        self.b = b
        self.par = at % 2
        self.next = 0 <= at + 1 < batches
        self.here = 0 <= at < batches
        self.layer1 = 0 <= at - 1 < batches
        self.layer2 = 0 <= at - 2 < batches
        self.after_next = at + 2 < batches


def steps(eng, batches, body):
    first, last = 2, 2 + (batches - 3) // 2 * 2
    for b in range(-1, first):
        body(Step(b, batches, None))
    with eng.Fori(first, last - 1, 2) as b:
        body(Step(b, batches, first))
        body(Step(b + 1, batches, first + 1))
    for b in range(last, batches + 2):
        body(Step(b, batches, None))


def build_program(nc, x, xT, adj, adjT, Wq, bq, Wk, bk, Wv, bv, Wo, bo, W1, a1, a2, out):
    B, N, D = x.shape
    H = 8
    HD = D // H
    NT = N // P
    FT = D // P
    G = FT
    HG = H // G
    UNITS = G * NT
    SCALE = float(HD) ** -0.5

    with ExitStack() as ctx:
        def sb(name, shape, dt=F32):
            return ctx.enter_context(nc.sbuf_tensor(name, shape, dt))

        def ps(name, shape, dt=F32):
            return ctx.enter_context(nc.psum_tensor(name, shape, dt))

        def sem(name):
            return ctx.enter_context(nc.semaphore(name))

        score_bank = [ps(f"score_bank{i}", [P, N]) for i in range(2)]
        a_bank = [ps(f"a_bank{i}", [P, N]) for i in range(2)]
        o_bank = [ps(f"o_bank{g}", [P, N]) for g in range(2)]
        m_bank = [ps(f"m_bank{i}", [P, N]) for i in range(2)]

        ident = sb("ident", [P, P])
        ident_bf = sb("ident_bf", [P, P], BF16)
        ones = sb("ones", [P, P])
        ones_r = sb("ones_r", [2, P], F32R)
        minus_half = sb("minus_half", [P, NT])
        wq_h, wq_l = sb("wq_h", [P, FT, D], F32R), sb("wq_l", [P, FT, D], F32R)
        wk_h, wk_l = sb("wk_h", [P, FT, D], F32R), sb("wk_l", [P, FT, D], F32R)
        wv_h, wv_l = sb("wv_h", [P, FT, D], F32R), sb("wv_l", [P, FT, D], F32R)
        wo = sb("wo", [P, FT, D])
        bq_col, bk_col = sb("bq_col", [P, FT]), sb("bk_col", [P, FT])
        bias_rows = sb("bias_rows", [2, 2, D], F32R)
        a_col = sb("a_col", [P, 2, FT])
        w12 = sb("w12", [P, 2, D])

        xT_in = sb("xT_in", [P, FT, N])
        xT_h, xT_l = sb("xT_h", [P, FT, N], F32R), sb("xT_l", [P, FT, N], F32R)
        q_h, q_l = sb("q_h", [P, N], F32R), sb("q_l", [P, N], F32R)
        k_h, k_l = sb("k_h", [P, N], F32R), sb("k_l", [P, N], F32R)
        KR = 3 * HD + 2
        q_st = [sb(f"q_st{i}", [P, H, N], F32R) for i in range(2)]
        k_st = [sb(f"k_st{i}", [P, H, N], F32R) for i in range(2)]
        v = [sb(f"v{i}", [P, NT, D]) for i in range(2)]
        adj_in = sb("adj_in", [P, NT, N], I32)
        sign = [sb(f"sign{i}", [P, NT, N], I8) for i in range(2)]
        mask_a = [sb(f"mask_a{i}", [P, NT, N], BF16) for i in range(2)]
        mask_t = [sb(f"mask_t{i}", [P, NT, N], BF16) for i in range(2)]
        mask_g = sb("mask_g", [P, NT, N], BF16)
        maxes = sb("maxes", [P, NT, H])
        m_parts = sb("m_parts", [32 + HG, N], F32R)
        m_h, m_l = m_parts[0:HG, :], m_parts[32:32 + HG, :]
        probs = [sb(f"probs{i}", [P, HG, N]) for i in range(2)]
        psums = sb("psums", [P, HG, N])
        oT = sb("oT", [P, G, N])
        rows = [sb(f"rows{i}", [P, NT, D]) for i in range(2)]
        stats1, stats2 = sb("stats1", [P, NT, 6]), sb("stats2", [P, NT, 6])
        mv1, mv2 = sb("mv1", [P, NT, 2]), sb("mv2", [P, NT, 2])
        ve1, ve2 = sb("ve1", [P, NT]), sb("ve2", [P, NT])
        rstd1, rstd2 = sb("rstd1", [P, NT]), sb("rstd2", [P, NT])
        nmean1, shift1 = sb("nmean1", [P, NT]), sb("shift1", [P, NT])
        f_col = sb("f_col", [P, 2, NT])
        f2_diag = sb("f2_diag", [P, NT, P])
        g_p = sb("g_p", [P, NT, N])
        g_pT = sb("g_pT", [P, NT, N])
        g_max, g_nmax = sb("g_max", [P, NT]), sb("g_nmax", [P, NT])
        g_sum, g_recip = sb("g_sum", [P, NT]), sb("g_recip", [P, NT])
        h1 = sb("h1", [P, NT, D])
        h1e = sb("h1e", [P, 2, D])

        brow = rows[0][0:1, 0:2, :]
        brow_h, brow_l = q_h[0:1, :], q_l[0:1, :]

        d_w, d_rows = sem("d_w"), sem("d_rows")
        d_xT, d_x, d_adj, d_adjT = sem("d_xT"), sem("d_x"), sem("d_adj"), sem("d_adjT")
        d_qst, d_kst, d_mrow, d_out = sem("d_qst"), sem("d_kst"), sem("d_mrow"), sem("d_out")
        c_pool, c_ident, c_dve, c_w12, c_w12sb = (sem("c_pool"), sem("c_ident"), sem("c_dve"), sem("c_w12"),
                                                  sem("c_w12sb"))
        qk_ready, v_ready = sem("qk_ready"), sem("v_ready")
        sa_ready, mT_ready, sb_ready = sem("sa_ready"), sem("mT_ready"), sem("sb_ready")
        pv_done, den_ready, wo_ready, f2_ready = sem("pv_done"), sem("den_ready"), sem("wo_ready"), sem("f2_ready")
        pT_ready, av_ready = sem("pT_ready"), sem("av_ready")
        xh_done, qkh_done, v_done = sem("xh_done"), sem("qkh_done"), sem("v_done")
        exp_done, mh_done = sem("exp_done"), sem("mh_done")
        gadd_done, gexp_done, pT_done, h_done, he_done = (sem("gadd_done"), sem("gexp_done"), sem("pT_done"),
                                                           sem("h_done"), sem("he_done"))
        qkl_done, sign_done, maska_done, maskg_done = (sem("qkl_done"), sem("sign_done"), sem("maska_done"),
                                                       sem("maskg_done"))
        max_done, ml_done, recip_done, o_done = sem("max_done"), sem("ml_done"), sem("recip_done"), sem("o_done")
        y_done, st1_done, mv1_done, x1_done = sem("y_done"), sem("st1_done"), sem("mv1_done"), sem("x1_done")
        leaky_done = sem("leaky_done")
        f_done, diag_done, gmax_done, gnmax_done, grecip_done = (sem("f_done"), sem("diag_done"), sem("gmax_done"),
                                                                 sem("gnmax_done"), sem("grecip_done"))
        z_done, y2_done, st2_done, mv2_done, outn_done = (sem("z_done"), sem("y2_done"), sem("st2_done"),
                                                          sem("mv2_done"), sem("outn_done"))
        xl_done, maskt_done, add_done = sem("xl_done"), sem("maskt_done"), sem("add_done")
        ve1_done, rstd1_done, hneg_done, ve2_done, rstd2_done = (sem("ve1_done"), sem("rstd1_done"),
                                                                 sem("hneg_done"), sem("ve2_done"),
                                                                 sem("rstd2_done"))

        held_dve, held_pool = sem("held_dve"), sem("held_pool")

        ADDS = 3 * H
        W_DMAS = 11
        IS_Q = (True, False, False, True)
        QK_BANK = (0, 1, 0, 1)

        def due(value):
            return not isinstance(value, int) or value > 0

        def hold(eng, spare):
            eng.sem_inc(spare, 1)

        block = ctx.enter_context(nc.Block())

        @block.sync
        def _(sp):
            sp.sem_inc(d_out, 16)
            sp.dma_start(g_p[:, 0, :].rearrange("p (c o) -> p c o", c=FT),
                         Wq.rearrange("(c p) o -> p c o", p=P)).then_inc(d_w, 16)
            sp.dma_start(g_p[:, 1, :].rearrange("p (c o) -> p c o", c=FT),
                         Wk.rearrange("(c p) o -> p c o", p=P)).then_inc(d_w, 16)
            sp.dma_start(g_p[:, 2, :].rearrange("p (c o) -> p c o", c=FT),
                         Wv.rearrange("(c p) o -> p c o", p=P)).then_inc(d_w, 16)
            sp.dma_start(g_p[:, 3, :].rearrange("p (c o) -> p c o", c=FT),
                         W1.rearrange("(c p) o -> p c o", p=P)).then_inc(d_w, 16)
            sp.dma_start(wo[:], Wo.rearrange("(c p) o -> p c o", p=P)).then_inc(d_w, 16)
            for col, vec in ((bq_col, bq), (bk_col, bk)):
                sp.dma_start(col[:], vec).then_inc(d_w, 16)
            sp.dma_start(a_col[:, 0, :], a1).then_inc(d_w, 16)
            sp.dma_start(a_col[:, 1, :], a2).then_inc(d_w, 16)
            sp.dma_start(brow[:, 0, :], bv.rearrange("(a d) -> a d", a=1)).then_inc(d_w, 16)
            sp.dma_start(brow[:, 1, :], bo.rearrange("(a d) -> a d", a=1)).then_inc(d_w, 16)
            sp.dma_start(xT_in[:], xT[0].rearrange("(c p) n -> p c n", p=P)).then_inc(d_xT, 16)
            sp.dma_start(adj_in[:], adj[0].rearrange("(t p) m -> p t m", p=P)).then_inc(d_adj, 16)
            sp.wait_ge(c_dve, 8)
            sp.dma_start(bias_rows[0:1, :, :].rearrange("p k d -> p (k d)").bitcast(F32), brow_h.bitcast(F32)).then_inc(d_rows, 16)
            sp.dma_start(bias_rows[1:2, :, :].rearrange("p k d -> p (k d)").bitcast(F32), brow_l.bitcast(F32)).then_inc(d_rows, 16)

            def body(s):
                b = s.b
                qs, ks = q_st[1 - s.par], k_st[1 - s.par]

                def stack(g):
                    mine = slice(g * HG, (g + 1) * HG)
                    for i in (2 * g, 2 * g + 1):
                        sp.wait_ge(qkl_done, (b + 1) * 2 * G + i + 1)
                        if IS_Q[i]:
                            sp.dma_start(qs[0:HD, mine, :].bitcast(F32), q_h[:].bitcast(F32)).then_inc(d_qst, 16)
                            sp.dma_start(qs[HD:2 * HD, mine, :].bitcast(F32), q_l[:].bitcast(F32)).then_inc(d_qst, 16)
                            sp.dma_start(qs[2 * HD:3 * HD, mine, :].bitcast(F32), q_h[:].bitcast(F32)).then_inc(d_qst, 16)
                        else:
                            sp.dma_start(ks[0:HD, mine, :].bitcast(F32), k_h[:].bitcast(F32)).then_inc(d_kst, 16)
                            sp.dma_start(ks[HD:2 * HD, mine, :].bitcast(F32), k_h[:].bitcast(F32)).then_inc(d_kst, 16)
                            sp.dma_start(ks[2 * HD:3 * HD, mine, :].bitcast(F32), k_l[:].bitcast(F32)).then_inc(d_kst, 16)

                if s.after_next:
                    sp.wait_ge(xh_done, b + 1 + 1)
                    sp.wait_ge(xl_done, b + 1 + 1)
                    sp.dma_start(xT_in[:], xT[b + 2].rearrange("(c p) n -> p c n", p=P)).then_inc(d_xT, 16)
                if s.next:
                    if due((b - 1) * H * NT + H * NT):
                        sp.wait_ge(sb_ready, (b - 1) * H * NT + H * NT)
                    stack(0)
                    sp.wait_ge(sign_done, b + 1 + 1)
                    sp.dma_start(adj_in[:], adjT[b + 1].rearrange("(t p) m -> p t m", p=P)).then_inc(d_adjT, 16)
                if s.here:
                    sp.wait_ge(ml_done, b * G + 2)
                    sp.dma_start(q_st[s.par][3 * HD:3 * HD + 1, HG:H, :].bitcast(F32),
                                 m_h[:].bitcast(F32)).then_inc(d_mrow, 16)
                    sp.dma_start(q_st[s.par][3 * HD + 1:KR, HG:H, :].bitcast(F32),
                                 m_l[:].bitcast(F32)).then_inc(d_mrow, 16)
                if s.after_next:
                    sp.wait_ge(maskt_done, b + 1 + 1)
                    sp.dma_start(adj_in[:], adj[b + 2].rearrange("(t p) m -> p t m", p=P)).then_inc(d_adj, 16)
                if s.next:
                    stack(1)
                    sp.wait_ge(ml_done, (b + 1) * G + 1)
                    sp.dma_start(qs[3 * HD:3 * HD + 1, 0:HG, :].bitcast(F32), m_h[:].bitcast(F32)).then_inc(d_mrow, 16)
                    sp.dma_start(qs[3 * HD + 1:KR, 0:HG, :].bitcast(F32), m_l[:].bitcast(F32)).then_inc(d_mrow, 16)
                if s.here:
                    if due((b - 2) * 2 + 2):
                        sp.wait_ge(y2_done, (b - 2) * 2 + 2)
                    sp.dma_start(rows[s.par][:], x[b].rearrange("(t p) d -> p t d", p=P)).then_inc(d_x, 16)
                if s.layer2:
                    sp.wait_ge(outn_done, (b - 2) * NT + NT)
                    sp.dma_start(out[b - 2].rearrange("(t p) d -> p t d", p=P), h1[:]).then_inc(d_out, 16)

            steps(sp, B, body)
            sp.wait_ge(d_out, 16 * (B + 1))

        @block.gpsimd
        def _(pool):
            pool.memset(ones[:], 1.0).then_inc(c_pool, 1)
            pool.memset(minus_half[:], -0.5).then_inc(c_pool, 1)
            pool.wait_ge(c_pool, 1)
            pool.affine_select(out=ident[:], in_=ones[:], compare_op=ALU.is_equal, fill=0.0, base=0,
                               pattern=[[-1, P]], channel_multiplier=1).then_inc(c_ident, 1)

            def split_xT(batch):
                pool.wait_ge(xh_done, batch + 1)
                if due((batch - 1) * 2 * G + 2 * G):
                    pool.wait_ge(qk_ready, (batch - 1) * 2 * G + 2 * G)
                pool.tensor_tensor(xT_l[:], xT_in[:], xT_h[:].bitcast(F32), ALU.subtract).then_inc(xl_done, 1)

            split_xT(0)

            def body(s):
                b = s.b

                def add_keys(u):
                    g, t = divmod(u, NT)
                    for j in range(HG):
                        pool.wait_ge(exp_done, b * H * NT + HG * u + j + 1)
                        if t == 1:
                            if j == 0:
                                if due(b * G + g):
                                    pool.wait_ge(den_ready, b * G + g)
                            pool.tensor_tensor(psums[:, j, :], probs[(u - 1) % 2][:, j, :],
                                               probs[u % 2][:, j, :], ALU.add).then_inc(add_done, 1)
                        else:
                            pool.wait_ge(add_done, b * ADDS + (g * 3 + t - 2) * HG + j + 1)
                            pool.tensor_tensor(psums[:, j, :], psums[:, j, :],
                                               probs[u % 2][:, j, :], ALU.add).then_inc(add_done, 1)

                if s.here:
                    add_keys(1)
                    add_keys(2)
                if s.layer1:
                    pool.wait_ge(mv1_done, (b - 1) * NT + NT)
                    hold(pool, held_pool)
                    pool.tensor_scalar(ve1[:], mv1[:, :, 1], EPS, 1.0, ALU.add, ALU.mult).then_inc(ve1_done, 1)
                    pool.tensor_scalar(nmean1[:], mv1[:, :, 0], -1.0, 1.0, ALU.mult, ALU.mult).then_inc(ve1_done, 1)
                    pool.wait_ge(ve1_done, (b - 1) * 2 + 2)
                    pool.tensor_tensor(rstd1[:], ve1[:], minus_half[:], ALU.pow).then_inc(rstd1_done, 1)
                    pool.wait_ge(rstd1_done, (b - 1) * 2 + 1)
                    pool.tensor_tensor(shift1[:], nmean1[:], rstd1[:], ALU.mult).then_inc(rstd1_done, 1)
                if s.here:
                    add_keys(3)
                if s.here:
                    add_keys(5)
                    add_keys(6)
                if s.after_next:
                    split_xT(b + 2)
                if s.here:
                    add_keys(7)
                if s.layer2:
                    pool.wait_ge(mv2_done, (b - 2) * NT + NT)
                    hold(pool, held_pool)
                    pool.tensor_scalar(ve2[:], mv2[:, :, 1], EPS, 1.0, ALU.add, ALU.mult).then_inc(ve2_done, 1)
                    pool.wait_ge(ve2_done, b - 2 + 1)
                    pool.tensor_tensor(rstd2[:], ve2[:], minus_half[:], ALU.pow).then_inc(rstd2_done, 1)
                    pool.wait_ge(rstd2_done, b - 2 + 1)
                    hold(pool, held_pool)
                    for t in range(NT):
                        pool.tensor_scalar(h1[:, t, :], h1[:, t, :], mv2[:, t, 0:1], rstd2[:, t:t + 1],
                                           ALU.subtract, ALU.mult).then_inc(outn_done, 1)

            steps(pool, B, body)

        @block.scalar
        def _(act):
            def split_xT(batch):
                act.wait_ge(d_xT, batch * 16 + 16)
                if due((batch - 1) * 2 * G + 2 * G):
                    act.wait_ge(qk_ready, (batch - 1) * 2 * G + 2 * G)
                act.copy(xT_h[:], xT_in[:]).then_inc(xh_done, 1)

            split_xT(0)

            def body(s):
                b = s.b

                def exp_chunk(u, j):
                    c = HG * u + j
                    if not s.here:
                        return
                    act.wait_ge(sb_ready, b * H * NT + c + 1)
                    if due(b * UNITS + u - 1):
                        act.wait_ge(pv_done, b * UNITS + u - 1)
                    g, t = divmod(u, NT)
                    if t == 0:
                        if due(b * ADDS + (g * 3 - 2) * HG + j + 1):
                            act.wait_ge(add_done, b * ADDS + (g * 3 - 2) * HG + j + 1)
                    elif t == 1:
                        if due(b * ADDS + (g * 3 - 1) * HG + j + 1):
                            act.wait_ge(add_done, b * ADDS + (g * 3 - 1) * HG + j + 1)
                    else:
                        act.wait_ge(add_done, b * ADDS + (g * 3 + t - 2) * HG + j + 1)
                    act.activation(probs[u % 2][:, j, :], score_bank[c % 2][:], ACT.Exp,
                                   scale=SCALE).then_inc(exp_done, 1)

                def high_part(i):
                    if not s.next:
                        return
                    g = i // 2
                    dst, col, d_st = (q_h, bq_col, d_qst) if IS_Q[i] else (k_h, bk_col, d_kst)
                    bank = m_bank[QK_BANK[i]]
                    act.wait_ge(qk_ready, (b + 1) * 2 * G + i + 1)
                    if due((b + 1) * 3 * 16 * G + 3 * 16 * g):
                        act.wait_ge(d_st, (b + 1) * 3 * 16 * G + 3 * 16 * g)
                    if due((b + 1) * 2 * G + 2 * g):
                        act.wait_ge(qkl_done, (b + 1) * 2 * G + 2 * g)
                    act.activation(dst[:], bank[:], ACT.Identity,
                                   bias=col[:, g:g + 1]).then_inc(qkh_done, 1)

                def evacuate_pT(t):
                    if not s.layer2:
                        return
                    act.wait_ge(pT_ready, (b - 2) * NT + t + 1)
                    act.copy(g_pT[:, t, :], m_bank[t % 2][:]).then_inc(pT_done, 1)

                def high_max(batch, g):
                    act.wait_ge(mT_ready, batch * G + g + 1)
                    if due(batch * 2 * 16 * G + 2 * 16 * g):
                        act.wait_ge(d_mrow, batch * 2 * 16 * G + 2 * 16 * g)
                    if due(batch * G + g):
                        act.wait_ge(ml_done, batch * G + g)
                    act.activation(m_h[:], m_bank[1][0:HG, :], ACT.Copy, scale=-1.0).then_inc(mh_done, 1)

                def take_v(i):
                    if not s.next:
                        return
                    act.wait_ge(v_ready, (b + 1) * 2 + i + 1)
                    if due((b - 1) * UNITS + UNITS):
                        act.wait_ge(pv_done, (b - 1) * UNITS + UNITS)
                    act.copy(v[1 - s.par][:, 2 * i:2 * i + 2, :],
                             m_bank[0][:].rearrange("p (t d) -> p t d", t=2)).then_inc(v_done, 1)

                def divide(i):
                    if not s.layer2:
                        return
                    act.wait_ge(grecip_done, b - 2 + 1)
                    act.wait_ge(av_ready, (b - 2) * 2 + i + 1)
                    for t in (2 * i, 2 * i + 1):
                        act.activation(h1[:, t, :], m_bank[i][:, (t % 2) * D:(t % 2 + 1) * D], ACT.Copy,
                                       scale=g_recip[:, t:t + 1]).then_inc(h_done, 1)

                def exp_negative(i):
                    if not s.layer2:
                        return
                    if i == 1:
                        act.wait_ge(z_done, (b - 2) * 2 + 1)
                    act.wait_ge(h_done, (b - 2) * NT + 2 * i + 2)
                    act.activation(h1e[:], h1[:, 2 * i:2 * i + 2, :], ACT.Relu, scale=-1.0).then_inc(hneg_done, 1)
                    act.wait_ge(hneg_done, (b - 2) * 2 + i + 1)
                    act.activation(h1e[:], h1e[:], ACT.Exp, scale=-1.0).then_inc(he_done, 1)

                def normalise1():
                    if not s.layer1:
                        return
                    x1 = rows[1 - s.par]
                    act.wait_ge(rstd1_done, (b - 1) * 2 + 2)
                    for t in range(NT):
                        act.activation(x1[:, t, :], x1[:, t, :], ACT.Identity, scale=rstd1[:, t:t + 1],
                                       bias=shift1[:, t:t + 1]).then_inc(x1_done, 1)

                for u in range(UNITS):
                    if u == 3 and s.here:
                        high_max(b, 1)
                    if u == 4:
                        if s.layer2:
                            act.wait_ge(d_out, (b - 2) * 16 + 16)
                        divide(0)
                    if u == 7 and s.next:
                        high_max(b + 1, 0)
                    exp_chunk(u, 0)
                    exp_chunk(u, 1)
                    if u == 0:
                        high_part(0)
                    if u == 2:
                        evacuate_pT(3)
                    if u == 4:
                        normalise1()
                        divide(1)
                    if u == 5 and s.layer1:
                        for t in range(NT):
                            act.wait_ge(f_done, (b - 1) * 2 * NT + 2 * NT)
                            act.activation(f2_diag[:, t, :], ident[:], ACT.Copy,
                                           scale=f_col[:, 1, t:t + 1]).then_inc(diag_done, 1)
                    if u == 5:
                        high_part(2)
                    if u == 7 and s.layer1:
                        for t in range(NT):
                            act.wait_ge(gmax_done, (b - 1) * NT + t + 1)
                            act.activation(g_p[:, t, :], g_p[:, t, :], ACT.Identity,
                                           bias=f_col[:, 0, t:t + 1]).then_inc(gadd_done, 1)
                    exp_chunk(u, 2)
                    exp_chunk(u, 3)
                    if u == 0:
                        high_part(1)
                    if u == 1:
                        evacuate_pT(0)
                        evacuate_pT(1)
                        evacuate_pT(2)
                    if u == 2:
                        take_v(0)
                    if u == 4:
                        take_v(1)
                        exp_negative(0)
                    if u == 5:
                        exp_negative(1)
                        high_part(3)
                    if u == 6 and s.after_next:
                        split_xT(b + 2)
                    if u == 7 and s.layer1:
                        act.wait_ge(gnmax_done, (b - 1) * 2 + 2)
                        for t in range(NT):
                            act.wait_ge(leaky_done, (b - 1) * NT + t + 1)
                            act.activation(g_p[:, t, :], g_p[:, t, :], ACT.Exp, bias=g_nmax[:, t:t + 1],
                                           accum_out=g_sum[:, t:t + 1]).then_inc(gexp_done, 1)

            steps(act, B, body)

        @block.vector
        def _(dve):
            dve.memset(ones_r[:].bitcast(F32), 1.0)
            dve.memset(k_st[0][3 * HD:KR, :, :].bitcast(F32), 1.0)
            dve.memset(k_st[1][3 * HD:KR, :, :].bitcast(F32), 1.0)
            dve.wait_ge(c_ident, 1)
            dve.tensor_copy(ident_bf[:], ident[:])
            dve.wait_ge(d_w, 16 * W_DMAS)
            pairs = []
            for n, (hi, lo) in enumerate(((wq_h, wq_l), (wk_h, wk_l), (wv_h, wv_l))):
                for c in range(FT):
                    src = g_p[:, n, c * D:(c + 1) * D]
                    if n < 2:
                        src = src.rearrange("p (g j d) -> p g d j", g=G, j=HG)
                        pairs.append((hi[:, c, :].rearrange("p (g d j) -> p g d j", g=G, j=HG),
                                      lo[:, c, :].rearrange("p (g d j) -> p g d j", g=G, j=HG), src))
                    else:
                        pairs.append((hi[:, c, :], lo[:, c, :], src))
            for hi, lo, src in pairs:
                dve.tensor_copy(hi, src)
            browf = brow.rearrange("p k d -> p (k d)")
            dve.tensor_copy(brow_h, browf).then_inc(c_dve, 1)
            dve.wait_ge(c_dve, 1)
            for hi, lo, src in pairs:
                dve.tensor_tensor(lo, src, hi.bitcast(F32), ALU.subtract).then_inc(c_dve, 1)
            dve.tensor_tensor(brow_l, browf, brow_h.bitcast(F32), ALU.subtract).then_inc(c_dve, 1)
            for k in range(2):
                for c in range(FT):
                    dve.tensor_scalar(f2_diag[:, 2 * k + c, :], ones[:], a_col[:, k, c:c + 1], None,
                                      ALU.mult).then_inc(c_dve, 1)
            dve.wait_ge(c_w12, 1)
            dve.tensor_copy(w12[:], m_bank[0][:].rearrange("p (k d) -> p k d", k=2)).then_inc(c_w12sb, 1)
            dve.wait_ge(c_w12sb, 1)

            def body(s):
                b = s.b

                def low_part(i):
                    g = i // 2
                    hi, lo, col, d_st = (q_h, q_l, bq_col, d_qst) if IS_Q[i] else (k_h, k_l, bk_col, d_kst)
                    dve.wait_ge(qkh_done, (b + 1) * 2 * G + i + 1)
                    if due((b + 1) * 3 * 16 * G + 3 * 16 * g):
                        dve.wait_ge(d_st, (b + 1) * 3 * 16 * G + 3 * 16 * g)
                    dve.scalar_tensor_tensor(out=lo[:], in0=m_bank[QK_BANK[i]][:], scalar=col[:, g:g + 1],
                                             in1=hi[:].bitcast(F32), op0=ALU.add,
                                             op1=ALU.subtract).then_inc(qkl_done, 1)

                def maxima(batch, first, last):
                    for n in range(first, last):
                        h, t = divmod(n, NT)
                        dve.wait_ge(sa_ready, batch * H * NT + n + 1)
                        hold(dve, held_dve)
                        dve.tensor_tensor_reduce(a_bank[n % 2][:], a_bank[n % 2][:],
                                                 mask_a[s.par if first >= 20 else 1 - s.par][:, t, :], 1.0, -3.0e38,
                                                 ALU.add, ALU.max, maxes[:, t, h:h + 1]).then_inc(max_done, 1)

                def pair(u, i):
                    n = 4 * u + 2 * i
                    if u < 3:
                        if s.here:
                            maxima(b, 20 + n, 22 + n)
                    elif s.next:
                        maxima(b + 1, n - 12, n - 10)

                def invert(batch, g, i):
                    cols = slice(i * N // 2, (i + 1) * N // 2)
                    if i == 0:
                        dve.wait_ge(den_ready, batch * G + g + 1)
                        if due((batch - 1) * 2 + 2):
                            dve.wait_ge(wo_ready, (batch - 1) * 2 + 2)
                    dve.reciprocal(oT[:, g, cols], m_bank[1 - g][:, cols]).then_inc(recip_done, 1)

                def normalised(batch, g):
                    dve.wait_ge(recip_done, batch * 2 * G + 2 * g + 2)
                    dve.wait_ge(pv_done, batch * UNITS + (g + 1) * NT)
                    dve.tensor_tensor(oT[:, g, :], o_bank[g][:], oT[:, g, :], ALU.mult).then_inc(o_done, 1)

                def low_max(batch, g):
                    dve.wait_ge(mh_done, batch * G + g + 1)
                    if due(batch * 2 * 16 * G + 2 * 16 * g):
                        dve.wait_ge(d_mrow, batch * 2 * 16 * G + 2 * 16 * g)
                    dve.scalar_tensor_tensor(out=m_l[:], in0=m_bank[1][0:HG, :], scalar=-1.0,
                                             in1=m_h[:].bitcast(F32), op0=ALU.mult,
                                             op1=ALU.subtract).then_inc(ml_done, 1)

                def residual(i):
                    if not s.layer1:
                        return
                    dve.wait_ge(d_x, (b - 1) * 16 + 16)
                    dve.wait_ge(wo_ready, (b - 1) * 2 + i + 1)
                    y = rows[1 - s.par]
                    dve.scalar_tensor_tensor(
                        out=y[:, 2 * i:2 * i + 2, :], in0=m_bank[i][:].rearrange("p (t d) -> p t d", t=2),
                        scalar=0.0, in1=y[:, 2 * i:2 * i + 2, :], op0=ALU.max, op1=ALU.add).then_inc(y_done, 1)

                def elu(i):
                    if not s.layer2:
                        return
                    half = slice(2 * i, 2 * i + 2)
                    x1 = rows[s.par]
                    dve.wait_ge(he_done, (b - 2) * 2 + i + 1)
                    dve.wait_ge(av_ready, (b - 2) * 2 + 2)
                    dve.scalar_tensor_tensor(out=x1[:, half, :], in0=h1e[:], scalar=-1.0, in1=x1[:, half, :],
                                             op0=ALU.add, op1=ALU.add).then_inc(z_done, 1)
                    dve.wait_ge(z_done, (b - 2) * 2 + i + 1)
                    dve.scalar_tensor_tensor(out=h1[:, half, :], in0=h1[:, half, :], scalar=0.0,
                                             in1=x1[:, half, :], op0=ALU.max, op1=ALU.add).then_inc(y2_done, 1)

                pair(0, 0)
                if s.next:
                    low_part(0)
                pair(0, 1)
                if s.layer1:
                    invert(b - 1, 1, 0)
                if s.next:
                    low_part(1)
                pair(1, 0)
                if s.layer1:
                    invert(b - 1, 1, 1)
                    normalised(b - 1, 1)
                if s.layer2:
                    dve.wait_ge(gexp_done, (b - 2) * NT + NT)
                    dve.reciprocal(g_recip[:], g_sum[:]).then_inc(grecip_done, 1)
                pair(1, 1)
                if s.layer1:
                    dve.tensor_scalar(mask_g[:], sign[1 - s.par][:], 0.0, NEG,
                                      ALU.is_equal, ALU.mult).then_inc(maskg_done, 1)
                if s.next:
                    dve.wait_ge(d_adj, (b + 1) * 16 + 16)
                    if due(b):
                        dve.wait_ge(maskg_done, b)
                    dve.tensor_scalar(sign[1 - s.par][:], adj_in[:], 1.0, -1.0,
                                      ALU.min, ALU.max).then_inc(sign_done, 1)
                pair(2, 0)
                if s.next:
                    dve.wait_ge(sign_done, b + 1 + 1)
                    dve.tensor_scalar(mask_a[1 - s.par][:], sign[1 - s.par][:], 0.0, NEG,
                                      ALU.is_le, ALU.mult).then_inc(maska_done, 1)
                residual(0)
                pair(2, 1)
                residual(1)
                if s.here:
                    low_max(b, 1)
                if s.next:
                    dve.wait_ge(maska_done, b + 1 + 1)
                pair(3, 0)
                if s.layer1:
                    y = rows[1 - s.par]
                    dve.wait_ge(y_done, (b - 1) * 2 + 2)
                    for t in range(NT):
                        dve.bn_stats(stats1[:, t, :], y[:, t, :]).then_inc(st1_done, 1)
                    dve.wait_ge(st1_done, (b - 1) * NT + NT)
                    hold(dve, held_dve)
                    for t in range(NT):
                        dve.bn_aggr(mv1[:, t, :], stats1[:, t, :]).then_inc(mv1_done, 1)
                pair(3, 1)
                if s.next:
                    dve.wait_ge(d_adjT, (b + 1) * 16 + 16)
                    if due((b - 1) * H * NT + H * NT):
                        dve.wait_ge(sb_ready, (b - 1) * H * NT + H * NT)
                    dve.tensor_scalar(mask_t[1 - s.par][:], adj_in[:], 0.0, NEG,
                                      ALU.is_le, ALU.mult).then_inc(maskt_done, 1)
                pair(4, 0)
                if s.layer1:
                    x1 = rows[1 - s.par]
                    dve.wait_ge(x1_done, (b - 1) * NT + NT)
                    if due(b - 2 + 1):
                        dve.wait_ge(f2_ready, b - 2 + 1)
                    for n in range(2 * NT):
                        k, t = divmod(n, NT)
                        if n >= 2:
                            dve.wait_ge(f_done, (b - 1) * 2 * NT + n - 1)
                        junk = f2_diag[:, 2 * (n % 2):2 * (n % 2) + 2, :].rearrange("p a b -> p (a b)")
                        dve.tensor_tensor_reduce(junk, x1[:, t, :], w12[:, k, :], 1.0, 0.0, ALU.mult, ALU.add,
                                                 f_col[:, k, t:t + 1]).then_inc(f_done, 1)
                pair(4, 1)
                if s.here:
                    invert(b, 0, 0)
                pair(5, 0)
                if s.here:
                    invert(b, 0, 1)
                    normalised(b, 0)
                elu(0)
                if s.next:
                    low_part(2)
                pair(5, 1)
                if s.next:
                    low_part(3)
                pair(6, 0)
                elu(1)
                pair(6, 1)
                if s.layer1:
                    if due((b - 2) * NT + NT):
                        dve.wait_ge(pT_ready, (b - 2) * NT + NT)
                    dve.wait_ge(f2_ready, b)
                    hold(dve, held_dve)
                    for t in range(NT):
                        dve.tensor_tensor_reduce(g_p[:, t, :], m_bank[0][:], mask_g[:, t, :], 1.0, -3.0e38,
                                                 ALU.add, ALU.max, g_max[:, t:t + 1]).then_inc(gmax_done, 1)
                if s.next:
                    low_max(b + 1, 0)
                pair(7, 0)
                if s.layer1:
                    dve.wait_ge(gmax_done, (b - 1) * NT + NT)
                    dve.scalar_tensor_tensor(out=g_max[:], in0=g_max[:], scalar=-1.0, in1=f_col[:, 0, :],
                                             op0=ALU.mult, op1=ALU.subtract).then_inc(gnmax_done, 1)
                    dve.wait_ge(gnmax_done, (b - 1) * 2 + 1)
                    dve.scalar_tensor_tensor(out=g_nmax[:], in0=g_max[:], scalar=ALPHA, in1=g_max[:],
                                             op0=ALU.mult, op1=ALU.min).then_inc(gnmax_done, 1)
                if s.layer1:
                    for t in (0, 1):
                        dve.wait_ge(gadd_done, (b - 1) * NT + t + 1)
                        dve.scalar_tensor_tensor(out=g_p[:, t, :], in0=g_p[:, t, :], scalar=ALPHA, in1=g_p[:, t, :],
                                                 op0=ALU.mult, op1=ALU.max).then_inc(leaky_done, 1)
                pair(7, 1)
                if s.layer1:
                    for t in (2, 3):
                        dve.wait_ge(gadd_done, (b - 1) * NT + t + 1)
                        dve.scalar_tensor_tensor(out=g_p[:, t, :], in0=g_p[:, t, :], scalar=ALPHA, in1=g_p[:, t, :],
                                                 op0=ALU.mult, op1=ALU.max).then_inc(leaky_done, 1)
                if s.layer2:
                    dve.wait_ge(y2_done, (b - 2) * 2 + 2)
                    for t in range(NT):
                        dve.bn_stats(stats2[:, t, :], h1[:, t, :]).then_inc(st2_done, 1)
                    dve.wait_ge(st2_done, (b - 2) * NT + NT)
                    hold(dve, held_dve)
                    for t in range(NT):
                        dve.bn_aggr(mv2[:, t, :], stats2[:, t, :]).then_inc(mv2_done, 1)

            steps(dve, B, body)

        @block.tensor
        def _(pe):
            pe.wait_ge(d_w, 16 * W_DMAS)
            pe.wait_ge(c_dve, 12)
            for k in range(2):
                for c in range(FT):
                    mm = pe.matmul(m_bank[0][:, k * D:(k + 1) * D], f2_diag[:, 2 * k + c, :],
                                   g_p[:, 3, c * D:(c + 1) * D], start=(c == 0), stop=(c == FT - 1))
            mm.then_inc(c_w12, 1)
            pe.wait_ge(c_w12sb, 1)
            pe.wait_ge(d_rows, 32)

            def body(s):
                b = s.b
                qn, kn = q_st[1 - s.par], k_st[1 - s.par]
                qs, ks = q_st[s.par], k_st[s.par]

                def scores(u, j):
                    if not s.here:
                        return
                    g, t = divmod(u, NT)
                    c, h = HG * u + j, g * HG + j
                    bank = score_bank[c % 2][:]
                    if j == 0:
                        pe.wait_ge(maskt_done, b + 1)
                        pe.wait_ge(d_mrow, b * 2 * 16 * G + 2 * 16 * (g + 1))
                    if due(b * H * NT + c - 1):
                        pe.wait_ge(exp_done, b * H * NT + c - 1)
                    pe.matmul(bank, ident_bf[:], mask_t[s.par][:, t, :], start=True, stop=False)
                    pe.matmul(bank, ks[0:KR, h, t * P:(t + 1) * P], qs[0:KR, h, :],
                              start=False, stop=True).then_inc(sb_ready, 1)

                def weigh(batch, par, u):
                    g, t = divmod(u, NT)
                    if t == 0:
                        pe.wait_ge(v_done, batch * 2 + 2)
                        if due((batch - 1) * G + g + 1):
                            pe.wait_ge(o_done, (batch - 1) * G + g + 1)
                    pe.wait_ge(exp_done, batch * H * NT + HG * (u + 1))
                    for j in range(HG):
                        h = g * HG + j
                        mm = pe.matmul(o_bank[g][HD * j:HD * (j + 1), :], v[par][:, t, h * HD:(h + 1) * HD],
                                       probs[u % 2][:, j, :], start=(t == 0), stop=(t == NT - 1))
                    mm.then_inc(pv_done, 1)

                def project(i):
                    g = i // 2
                    bank = m_bank[QK_BANK[i]][:]
                    wh, wl = (wq_h, wq_l) if IS_Q[i] else (wk_h, wk_l)
                    n = 0
                    for c in range(FT):
                        for w, xx in ((wh, xT_h), (wh, xT_l), (wl, xT_h)):
                            n += 1
                            mm = pe.matmul(bank, w[:, c, g * P:(g + 1) * P], xx[:, c, :],
                                           start=(n == 1), stop=(n == 3 * FT))
                    mm.then_inc(qk_ready, 1)

                def project_v(i):
                    for t in (2 * i, 2 * i + 1):
                        dst = m_bank[0][:, (t % 2) * D:(t % 2 + 1) * D]
                        pe.matmul(dst, ones_r[:], bias_rows[:, 0, :], start=True, stop=False)
                        n = 0
                        for c in range(FT):
                            for xx, w in ((xT_h, wv_h), (xT_l, wv_h), (xT_h, wv_l)):
                                n += 1
                                mm = pe.matmul(dst, xx[:, c, t * P:(t + 1) * P], w[:, c, :],
                                               start=False, stop=(n == 3 * FT))
                    mm.then_inc(v_ready, 1)

                def denominators(batch, g):
                    pe.wait_ge(add_done, batch * ADDS + (g + 1) * 3 * HG)
                    for j in range(HG):
                        mm = pe.matmul(m_bank[1 - g][HD * j:HD * (j + 1), :], ones[:, 0:HD], psums[:, j, :],
                                       start=True, stop=True)
                    mm.then_inc(den_ready, 1)

                def row_scores(batch, first, last):
                    q, k = (qs, ks) if first >= 20 else (qn, kn)
                    for n in range(first, last):
                        h, t = divmod(n, NT)
                        if t == 0 and h % HG == 0:
                            pe.wait_ge(d_qst, batch * 3 * 16 * G + 3 * 16 * (h // HG + 1))
                            pe.wait_ge(d_kst, batch * 3 * 16 * G + 3 * 16 * (h // HG + 1))
                        if due(batch * H * NT + n - 1):
                            pe.wait_ge(max_done, batch * H * NT + n - 1)
                        pe.matmul(a_bank[n % 2][:], q[0:3 * HD, h, t * P:(t + 1) * P], k[0:3 * HD, h, :],
                                  start=True, stop=True).then_inc(sa_ready, 1)

                def pair(u, i):
                    n = 4 * u + 2 * i
                    if u < 3:
                        if s.here:
                            row_scores(b, 20 + n, 22 + n)
                    elif s.next:
                        row_scores(b + 1, n - 12, n - 10)

                def turn_max(batch, g):
                    pe.wait_ge(max_done, batch * H * NT + (g + 1) * HG * NT)
                    for t in range(NT):
                        mm = pe.transpose(m_bank[1][0:HG, t * P:(t + 1) * P],
                                          maxes[:, t, g * HG:(g + 1) * HG], ident[:])
                    mm.then_inc(mT_ready, 1)

                def turn_graph(t):
                    for r in range(NT):
                        mm = pe.transpose(m_bank[t % 2][:, r * P:(r + 1) * P], g_p[:, r, t * P:(t + 1) * P], ident[:])
                    mm.then_inc(pT_ready, 1)

                def graph_sum(i):
                    x1 = rows[s.par]
                    pe.wait_ge(pT_done, (b - 2) * NT + NT)
                    for r in (2 * i, 2 * i + 1):
                        for t in range(NT):
                            mm = pe.matmul(m_bank[i][:, (r % 2) * D:(r % 2 + 1) * D],
                                           g_pT[:, t, r * P:(r + 1) * P], x1[:, t, :],
                                           start=(t == 0), stop=(t == NT - 1))
                    mm.then_inc(av_ready, 1)

                def output_projection(i):
                    for t in (2 * i, 2 * i + 1):
                        dst = m_bank[i][:, (t % 2) * D:(t % 2 + 1) * D]
                        pe.matmul(dst, ones_r[:], bias_rows[:, 1, :], start=True, stop=False)
                        for g in range(G):
                            mm = pe.matmul(dst, oT[:, g, t * P:(t + 1) * P], wo[:, g, :],
                                           start=False, stop=(g == G - 1))
                    mm.then_inc(wo_ready, 1)

                for u in range(UNITS):
                    if u == 3 and s.here:
                        if s.layer1:
                            pe.wait_ge(y_done, (b - 1) * 2 + 2)
                        else:
                            pe.wait_ge(qkl_done, (b + 1) * 2 * G + 2)
                        turn_max(b, 1)
                    if u == 7 and s.next:
                        pe.wait_ge(qkl_done, (b + 1) * 2 * G + 4)
                        turn_max(b + 1, 0)
                    scores(u, 0)
                    scores(u, 1)
                    pair(u, 0)
                    if u == 0 and s.next:
                        pe.wait_ge(xh_done, b + 1 + 1)
                        pe.wait_ge(xl_done, b + 1 + 1)
                        if due((b - 2) * NT + NT):
                            pe.wait_ge(gmax_done, (b - 2) * NT + NT)
                        if due(b * 2 * G + 3):
                            pe.wait_ge(qkl_done, b * 2 * G + 3)
                        project(0)
                    if u == 2 and s.layer2:
                        pe.wait_ge(pT_done, (b - 2) * NT + 2)
                        turn_graph(3)
                    if u == 2 and s.layer1:
                        pe.wait_ge(o_done, (b - 1) * G + G)
                        if due((b - 2) * NT + 3):
                            pe.wait_ge(pT_done, (b - 2) * NT + 3)
                        output_projection(0)
                    if u == 4 and s.layer2:
                        if s.here:
                            pe.wait_ge(ml_done, b * G + 2)
                        elif s.layer1:
                            pe.wait_ge(y_done, (b - 1) * 2 + 2)
                        graph_sum(1)
                    if u == 5 and s.next:
                        pe.wait_ge(v_done, (b + 1) * 2 + 2)
                        project(2)
                    if u == 6 and s.layer1:
                        pe.wait_ge(diag_done, (b - 1) * NT + NT)
                        if s.next:
                            pe.wait_ge(qkl_done, (b + 1) * 2 * G + 3)
                        else:
                            pe.wait_ge(h_done, (b - 2) * NT + 2)
                        pe.matmul(m_bank[0][:], ones[:], f2_diag[:].rearrange("p t n -> p (t n)"),
                                  start=True, stop=True).then_inc(f2_ready, 1)
                    scores(u, 2)
                    scores(u, 3)
                    pair(u, 1)
                    if u == 0:
                        if s.layer1:
                            weigh(b - 1, 1 - s.par, UNITS - 1)
                            if s.next:
                                pe.wait_ge(qkl_done, (b + 1) * 2 * G + 1)
                            else:
                                pe.wait_ge(gmax_done, (b - 2) * NT + NT)
                            denominators(b - 1, 1)
                    elif s.here:
                        weigh(b, s.par, u - 1)
                    if u == 0 and s.next:
                        if due(b * G + 1):
                            pe.wait_ge(ml_done, b * G + 1)
                        project(1)
                    if u == 1 and s.layer2:
                        pe.wait_ge(gexp_done, (b - 2) * NT + NT)
                        if s.layer1:
                            pe.wait_ge(recip_done, (b - 1) * 2 * G + 4)
                        else:
                            pe.wait_ge(gmax_done, (b - 2) * NT + NT)
                        turn_graph(0)
                    if u == 1 and s.layer2:
                        if s.next:
                            pe.wait_ge(qkl_done, (b + 1) * 2 * G + 2)
                        elif s.here:
                            pe.wait_ge(ml_done, b * G + 1)
                        elif s.layer1:
                            pe.wait_ge(recip_done, (b - 1) * 2 * G + 2)
                        else:
                            pe.wait_ge(h_done, (b - 3) * NT + NT)
                        turn_graph(1)
                        pe.wait_ge(pT_done, (b - 2) * NT + 1)
                        turn_graph(2)
                    if u == 2 and s.layer1:
                        if due((b - 2) * NT + 4):
                            pe.wait_ge(pT_done, (b - 2) * NT + 4)
                        if not s.layer2:
                            pe.wait_ge(qkl_done, (b + 1) * 2 * G + 2)
                        output_projection(1)
                    if u == 2 and s.next:
                        if s.layer1:
                            pe.wait_ge(y_done, (b - 1) * 2 + 1)
                        else:
                            pe.wait_ge(qkl_done, (b + 1) * 2 * G + 1)
                        project_v(0)
                    if u == 3 and s.layer2:
                        if s.next:
                            pe.wait_ge(v_done, (b + 1) * 2 + 1)
                        elif s.layer1:
                            pe.wait_ge(y_done, (b - 1) * 2 + 1)
                        graph_sum(0)
                    if u == 4 and s.here:
                        if s.layer2:
                            pe.wait_ge(h_done, (b - 2) * NT + NT)
                        else:
                            pe.wait_ge(ml_done, b * G + 2)
                        denominators(b, 0)
                    if u == 4 and s.next:
                        if s.layer2:
                            pe.wait_ge(h_done, (b - 2) * NT + 2)
                        else:
                            pe.wait_ge(v_done, (b + 1) * 2 + 1)
                        project_v(1)
                    if u == 5 and s.next:
                        if s.here:
                            pe.wait_ge(recip_done, b * 2 * G + 2)
                        else:
                            pe.wait_ge(qkl_done, (b + 1) * 2 * G + 2)
                        project(3)

            steps(pe, B, body)


def kernel(x, adj, L0_gnn_Wq, L0_gnn_bq, L0_gnn_Wk, L0_gnn_bk, L0_gnn_Wv, L0_gnn_bv, L0_gnn_Wo, L0_gnn_bo,
           L1_gnn_W, L1_gnn_a1, L1_gnn_a2):
    import numpy as np
    import concourse.bacc as bacc
    from concourse.bass_utils import run_bass_kernel_spmd

    x, adj = np.asarray(x), np.asarray(adj)

    def by_dim(vec):
        return np.asarray(vec).reshape(2, 4, 32).transpose(2, 1, 0).reshape(128, 2)

    def by_tile(vec):
        return np.asarray(vec).reshape(2, 128).T

    given = {
        "x": x, "xT": x.transpose(0, 2, 1), "adj": adj, "adjT": adj.transpose(0, 2, 1),
        "Wq": L0_gnn_Wq, "bq": by_dim(L0_gnn_bq), "Wk": L0_gnn_Wk, "bk": by_dim(L0_gnn_bk),
        "Wv": L0_gnn_Wv, "bv": L0_gnn_bv, "Wo": L0_gnn_Wo, "bo": L0_gnn_bo,
        "W1": L1_gnn_W, "a1": by_tile(L1_gnn_a1), "a2": by_tile(L1_gnn_a2),
    }
    nc = bacc.Bacc("TRN2", target_bir_lowering=False, num_devices=1)
    arrays, args = {}, []
    for name, value in given.items():
        a = np.ascontiguousarray(value)
        arrays[f"in_{name}"] = a
        args.append(nc.dram_tensor(f"in_{name}", a.shape, mybir.dt.from_np(a.dtype), kind="ExternalInput").ap())
    out = nc.dram_tensor("out_x", x.shape, F32, kind="ExternalOutput").ap()
    build_program(nc, *args, out)
    r = run_bass_kernel_spmd(nc, [arrays], core_ids=[0])
    return r.results[0]["out_x"]
```
